# Optimizing a Trainium2 kernel written in Bass

```python
import numpy as np
import jax
import jax.numpy as jnp

def _softmax(x, axis=-1):
    return jax.nn.softmax(x, axis=axis)

def _gelu(x):
    return jax.nn.gelu(x, approximate=True)

def _silu(x):
    return jax.nn.silu(x)

def _sigmoid(x):
    return jax.nn.sigmoid(x)

def _layernorm(x, axis=-1, eps=1e-05):
    m = jnp.mean(x, axis=axis, keepdims=True)
    v = jnp.var(x, axis=axis, keepdims=True)
    return (x - m) / jnp.sqrt(v + eps)

def _scatter_add(tgt, idx, src, axis=0):
    return tgt.at[idx].add(src)

def _segment_sum(src, seg, n):
    return jax.ops.segment_sum(src, seg, n)
kernel_name = 'mk_gnn_preln_d1_gnn_r32_904e82'

def setup_inputs(seed: int=0):
    np.random.seed(seed)
    _w = jnp.asarray

    def _rec_inputs():
        import jax
        import jax.numpy as jnp
        _gk = jax.random.key(seed)
        x = -0.000202 + 1 * jax.random.normal(jax.random.fold_in(_gk, 1), (50000, 128), jnp.float32)
        src = jax.random.randint(jax.random.fold_in(_gk, 2), (25000,), 0, 50000, jnp.int32)
        dst = jax.random.randint(jax.random.fold_in(_gk, 3), (25000,), 0, 50000, jnp.int32)
        _o = jnp.argsort(dst, stable=True)
        src = src[_o]
        dst = dst[_o]
        edge_attr_128 = -9.77346e-05 + 0.999888 * jax.random.normal(jax.random.fold_in(_gk, 12), (25000, 128), jnp.float32)
        return (x, src, dst, edge_attr_128)
    x, src, dst, edge_attr_128 = _rec_inputs()

    def _L0_gnn_setup():
        import jax, jax.numpy as jnp
        import numpy as np
        N, E = (50000, 12500)
        OBJ_D, REL_D, EFF_D, HID = (128, 128, 128, 256)

        def _mlp_params(key, in_d, hid, out_d, scale=0.02):
            k1, k2 = jax.random.split(key)
            return (jax.random.normal(k1, (in_d, hid), jnp.float32) * scale, jnp.zeros((hid,), jnp.float32), jax.random.normal(k2, (hid, out_d), jnp.float32) * scale, jnp.zeros((out_d,), jnp.float32))

        def _mlp(x, w1, b1, w2, b2):
            h = jax.nn.relu(x @ w1 + b1)
            return h @ w2 + b2
        key = jax.random.key(seed)
        ks = jax.random.split(key, 7)
        objects = jax.random.normal(ks[0], (N, OBJ_D), jnp.float32)
        relations = jax.random.normal(ks[1], (E, REL_D), jnp.float32)
        senders = jax.random.randint(ks[2], (E,), 0, N, jnp.int32)
        receivers = jax.random.randint(ks[3], (E,), 0, N, jnp.int32)
        re_w1, re_b1, re_w2, re_b2 = _mlp_params(ks[4], 2 * OBJ_D + REL_D, HID, EFF_D)
        oe_w1, oe_b1, oe_w2, oe_b2 = _mlp_params(ks[5], OBJ_D, HID, EFF_D)
        ea_w1, ea_b1, ea_w2, ea_b2 = _mlp_params(ks[6], EFF_D + OBJ_D, HID, OBJ_D)
        return dict(objects=objects, relations=relations, senders=senders, receivers=receivers, re_w1=re_w1, re_b1=re_b1, re_w2=re_w2, re_b2=re_b2, oe_w1=oe_w1, oe_b1=oe_b1, oe_w2=oe_w2, oe_b2=oe_b2, ea_w1=ea_w1, ea_b1=ea_b1, ea_w2=ea_w2, ea_b2=ea_b2)
    _L0_gnn_all = _L0_gnn_setup()
    _L0_gnn_in = {k: v for k, v in _L0_gnn_all.items() if k in ('re_w1', 're_b1', 're_w2', 're_b2', 'oe_w1', 'oe_b1', 'oe_w2', 'oe_b2', 'ea_w1', 'ea_b1', 'ea_w2', 'ea_b2')}
    del _L0_gnn_all
    return {'x': x, 'src': src, 'dst': dst, 'edge_attr_128': edge_attr_128, 'L0_gnn_re_w1': _L0_gnn_in['re_w1'], 'L0_gnn_re_b1': _L0_gnn_in['re_b1'], 'L0_gnn_re_w2': _L0_gnn_in['re_w2'], 'L0_gnn_re_b2': _L0_gnn_in['re_b2'], 'L0_gnn_oe_w1': _L0_gnn_in['oe_w1'], 'L0_gnn_oe_b1': _L0_gnn_in['oe_b1'], 'L0_gnn_oe_w2': _L0_gnn_in['oe_w2'], 'L0_gnn_oe_b2': _L0_gnn_in['oe_b2'], 'L0_gnn_ea_w1': _L0_gnn_in['ea_w1'], 'L0_gnn_ea_b1': _L0_gnn_in['ea_b1'], 'L0_gnn_ea_w2': _L0_gnn_in['ea_w2'], 'L0_gnn_ea_b2': _L0_gnn_in['ea_b2']}

def reference(x, src, dst, edge_attr_128, L0_gnn_re_w1, L0_gnn_re_b1, L0_gnn_re_w2, L0_gnn_re_b2, L0_gnn_oe_w1, L0_gnn_oe_b1, L0_gnn_oe_w2, L0_gnn_oe_b2, L0_gnn_ea_w1, L0_gnn_ea_b1, L0_gnn_ea_w2, L0_gnn_ea_b2):
    import jax
    import jax.numpy as jnp

    def _L0_gnn_ref(objects, relations, senders, receivers, re_w1, re_b1, re_w2, re_b2, oe_w1, oe_b1, oe_w2, oe_b2, ea_w1, ea_b1, ea_w2, ea_b2):
        import jax, jax.numpy as jnp
        import numpy as np
        N, E = (50000, 12500)
        OBJ_D, REL_D, EFF_D, HID = (128, 128, 128, 256)

        def _mlp_params(key, in_d, hid, out_d, scale=0.02):
            k1, k2 = jax.random.split(key)
            return (jax.random.normal(k1, (in_d, hid), jnp.float32) * scale, jnp.zeros((hid,), jnp.float32), jax.random.normal(k2, (hid, out_d), jnp.float32) * scale, jnp.zeros((out_d,), jnp.float32))

        def _mlp(x, w1, b1, w2, b2):
            h = jax.nn.relu(x @ w1 + b1)
            return h @ w2 + b2
        _obj_enc = _mlp(objects, oe_w1, oe_b1, oe_w2, oe_b2)
        rel_inputs = jnp.concatenate([objects[senders], objects[receivers], relations], axis=-1)
        rel_effects = _mlp(rel_inputs, re_w1, re_b1, re_w2, re_b2)
        agg_effects = jax.ops.segment_sum(rel_effects, receivers, num_segments=objects.shape[0])
        effect_inputs = jnp.concatenate([objects, agg_effects], axis=-1)
        updated_objects = _mlp(effect_inputs, ea_w1, ea_b1, ea_w2, ea_b2)
        return updated_objects
    h = jnp.maximum(_layernorm(x, axis=-1), 0.0)
    x = x + _L0_gnn_ref(h, edge_attr_128, src, dst, L0_gnn_re_w1, L0_gnn_re_b1, L0_gnn_re_w2, L0_gnn_re_b2, L0_gnn_oe_w1, L0_gnn_oe_b1, L0_gnn_oe_w2, L0_gnn_oe_b2, L0_gnn_ea_w1, L0_gnn_ea_b1, L0_gnn_ea_w2, L0_gnn_ea_b2)
    return x

_drawn_inputs = setup_inputs


def setup_inputs(seed=0):
    import zlib

    import numpy as np

    out = dict(_drawn_inputs(seed))
    spreads = {'L0_gnn_re_b1': (0.0, 0.8),
     'L0_gnn_re_b2': (0.0, 2.0),
     'L0_gnn_oe_b1': (0.0, 0.1),
     'L0_gnn_oe_b2': (0.0, 0.1),
     'L0_gnn_ea_b1': (0.0, 0.404),
     'L0_gnn_ea_b2': (0.0, 0.1)}
    factors = {'edge_attr_128': 8.0, 'L0_gnn_re_w1': 8.0, 'L0_gnn_re_w2': 8.0}
    for name, (base, spread) in spreads.items():
        noise = np.random.default_rng([zlib.crc32(name.encode()), seed]).standard_normal(out[name].shape)
        drawn = base * np.exp(spread * noise) if base else spread * noise
        out[name] = jnp.asarray(drawn.astype(out[name].dtype))
    for name, factor in factors.items():
        out[name] = (out[name] * factor).astype(out[name].dtype)
    return out
```

```python
import concourse.bass as bass
from concourse import mybir
from contextlib import ExitStack

P = 128
F32 = mybir.dt.float32
I32 = mybir.dt.int32
ALU = mybir.AluOpType
ACT = mybir.ActivationFunctionType
AX = mybir.AxisListType


def gnn_program(nc, x, src, dst, ea, re_w1, re_b1, re_w2, re_b2, ea_w1, ea_b1, ea_w2, ea_b2, out):
    N, D = x.shape
    E = src.shape[0]
    HID = re_w1.shape[1]
    C = HID // P
    T = 4
    G = T * P
    EG = E // G
    EDGE_TAIL = E - G
    DONE = (EG * G - EDGE_TAIL) // T
    NP = N // (2 * G)
    NODE_TAIL = N - 2 * G
    SPARE = N
    EPS = 1e-5
    LOADS = 16 * (4 + 2 * C + 2)
    assert (EG * G - EDGE_TAIL) % T == 0 and D == P and EG * G < E and NP * 2 * G < N

    agg = nc.dram_tensor("agg", [N + P, D], F32, kind="Internal").ap()

    ctx = ExitStack()
    with ctx:
        def sb(name, shape, dt=F32):
            return ctx.enter_context(nc.sbuf_tensor(name, shape, dt))

        def ps(name, shape):
            return ctx.enter_context(nc.psum_tensor(name, shape, F32))

        def sem(name):
            return ctx.enter_context(nc.semaphore(name))

        w1e = sb("w1e", [P, 3, HID])
        w2e = sb("w2e", [P, C, D])
        w1n = sb("w1n", [P, 2, HID])
        w2n = sb("w2n", [P, C, D])
        b1e = sb("b1e", [P, C])
        b1n = sb("b1n", [P, C])
        b2e = sb("b2e", [P, D])
        b2n = sb("b2n", [P, D])
        ident = sb("ident", [P, P])
        before = sb("before", [P, P])
        spare = sb("spare", [P, 1])
        eps = sb("eps", [P, 1])
        zeros = sb("zeros", [P, 2000])
        src_all = sb("src_all", [P, EG + 1, T], I32)
        dst_all = sb("dst_all", [P, EG + 1, T], I32)
        gidx = sb("gidx", [P, 2, T], I32)
        sidx = sb("sidx", [P, T], I32)
        gath = sb("gath", [P, 2, T, D])
        ea_in = sb("ea_in", [P, T, D])
        dstf = sb("dstf", [P, T])
        same = sb("same", [P, T, P])
        junk = sb("junk", [P, T, P])
        dup = sb("dup", [P, T])
        dups = sb("dups", [P, T])
        off = sb("off", [P, T])
        off2 = sb("off2", [P, T])
        rel = sb("rel", [P, T, D])
        relsum = sb("relsum", [P, T, D])
        tiles = [2 * T, T, T]
        h = [sb(f"h{r}", [P, tiles[r], D]) for r in range(3)]
        st = [sb(f"st{r}", [P, tiles[r], 6]) for r in range(3)]
        mv = [sb(f"mv{r}", [P, tiles[r], 2]) for r in range(3)]
        sd = [sb(f"sd{r}", [P, tiles[r]]) for r in range(3)]
        rs = [sb(f"rs{r}", [P, tiles[r]]) for r in range(3)]
        inT = [sb(f"inT{r}", [P, 3 if r == 0 else 2, G]) for r in range(3)]
        hid = [sb(f"hid{r}", [P, C, G]) for r in range(3)]
        xin = [None] + [sb(f"xin{r}", [P, T, D]) for r in (1, 2)]
        xb = [None] + [sb(f"xb{r}", [P, T, D]) for r in (1, 2)]
        agg_in = [None] + [sb(f"agg_in{r}", [P, T, D]) for r in (1, 2)]
        res = [None] + [sb(f"res{r}", [P, T, D]) for r in (1, 2)]

        tps = [ps(f"tps{b}", [P, G]) for b in range(3)]
        rowps = ps("rowps", [P, G])
        l1ps = [ps(f"l1ps{c}", [P, G]) for c in range(C)]
        l2ps = ps("l2ps", [P, G])
        sumps = ps("sumps", [P, G])

        loaded = sem("loaded")
        idx_loaded = sem("idx_loaded")
        consts = sem("consts")
        zeroed = sem("zeroed")
        zeros_set = sem("zeros_set")
        gidx_set = sem("gidx_set")
        gathered = [sem(f"gathered{k}") for k in range(T)]
        ea_loaded = sem("ea_loaded")
        ea_used = sem("ea_used")
        scattered = sem("scattered")
        dst_cast = sem("dst_cast")
        same_set = sem("same_set")
        dup_set = sem("dup_set")
        off_set = sem("off_set")
        off2_set = sem("off2_set")
        sidx_set = sem("sidx_set")
        summed = sem("summed")
        relsum_set = sem("relsum_set")
        stats = [sem(f"stats{r}") for r in range(3)]
        moments = [sem(f"moments{r}") for r in range(3)]
        deviation = [sem(f"deviation{r}") for r in range(3)]
        inverse = [sem(f"inverse{r}") for r in range(3)]
        normed = [sem(f"normed{r}") for r in range(3)]
        transposed = [sem(f"transposed{r}") for r in range(3)]
        inT_act = [sem(f"inT_act{r}") for r in range(3)]
        inT_dve = [sem(f"inT_dve{r}") for r in range(3)]
        l1_done = sem("l1_done")
        hid_set = sem("hid_set")
        l2_done = sem("l2_done")
        results = sem("results")
        tail_cast = sem("tail_cast")
        pool_passed = sem("pool_passed")
        dve_passed = sem("dve_passed")
        x_loaded = [None] + [sem(f"x_loaded{r}") for r in (1, 2)]
        xb_set = [None] + [sem(f"xb_set{r}") for r in (1, 2)]
        agg_loaded = [None] + [sem(f"agg_loaded{r}") for r in (1, 2)]
        agg_used = [None] + [sem(f"agg_used{r}") for r in (1, 2)]
        stored = [None] + [sem(f"stored{r}") for r in (1, 2)]

        def rows(t, start):
            return t[bass.ds(start, G), :].rearrange("(p k) f -> p k f", k=T)

        def wait(eng, s, value):
            if not isinstance(value, int) or value > 0:
                eng.wait_ge(s, value)

        block = ctx.enter_context(nc.Block())

        @block.sync
        def _(sp):
            for side, t in ((src, src_all), (dst, dst_all)):
                whole = side[0:EG * G].rearrange("(g p k) -> p g k", p=P, k=T)
                sp.dma_start(t[:, 1:EG + 1, :], whole).then_inc(idx_loaded, 16)
                sp.dma_start(t[:, 0, :], side[EDGE_TAIL:E].rearrange("(p k) -> p k", k=T)).then_inc(idx_loaded, 16)
            for t, w in ((w1e, re_w1), (w2e, re_w2), (w1n, ea_w1), (w2n, ea_w2)):
                sp.dma_start(t[:, :, :], w.rearrange("(c p) n -> p c n", p=P)).then_inc(loaded, 16)
            for t, b in ((b1e, re_b1), (b1n, ea_b1)):
                for c in range(C):
                    sp.dma_start(t[:, c:c + 1], b[c * P:(c + 1) * P].unsqueeze(1)).then_inc(loaded, 16)
            for t, b in ((b2e, re_b2), (b2n, ea_b2)):
                sp.dma_start(t[:, :], b.rearrange("(a n) -> a n", a=1).to_broadcast([P, D])).then_inc(loaded, 16)

            def load_ea(i, start):
                wait(sp, ea_used, i)
                sp.dma_start(ea_in[:, :, :], rows(ea, start)).then_inc(ea_loaded, 16)

            def load_nodes(j, start, edges):
                for r in (1, 2):
                    at = start + (r - 1) * G
                    wait(sp, normed[r], j * T)
                    wait(sp, xb_set[r], j)
                    sp.dma_start(xin[r][:, :, :], rows(x, at)).then_inc(x_loaded[r], 16)
                    wait(sp, scattered, 16 * T * edges)
                    wait(sp, agg_used[r], j)
                    sp.dma_start(agg_in[r][:, :, :], rows(agg, at)).then_inc(agg_loaded[r], 16)

            def store_nodes(start, u, overlapped=0):
                for r in (1, 2):
                    sp.wait_ge(results, u + r)
                    for other in (1, 2) if overlapped else ():
                        sp.wait_ge(stored[other], 16 * overlapped)
                    sp.dma_start(rows(out, start + (r - 1) * G), res[r][:, :, :]).then_inc(stored[r], 16)

            load_ea(0, EDGE_TAIL)
            with sp.Fori(0, EG) as e:
                load_ea(e + 1, e * G)
            load_nodes(0, 0, EG + 1)
            load_nodes(1, 2 * G, EG + 1)
            store_nodes(0, EG + 1)
            with sp.Fori(1, NP - 1) as j:
                load_nodes(j + 1, (j + 1) * 2 * G, EG + 1)
                store_nodes(j * 2 * G, EG + 1 + 2 * j)
            load_nodes(NP, NODE_TAIL, EG + 1)
            store_nodes((NP - 1) * 2 * G, EG + 1 + 2 * (NP - 1))
            store_nodes(NODE_TAIL, EG + 1 + 2 * NP, NP)
            for r in (1, 2):
                sp.wait_ge(stored[r], 16 * (NP + 1))

        @block.gpsimd
        def _(pool):
            nc.gpsimd.memset(zeros[:, :], 0.0).then_inc(zeros_set, 1)
            nc.gpsimd.memset(ident[:, :], 0.0).then_inc(consts, 1)
            nc.gpsimd.memset(before[:, :], 1.0).then_inc(consts, 1)
            nc.gpsimd.memset(eps[:, :], EPS).then_inc(consts, 1)
            nc.gpsimd.iota(spare[:, :], pattern=[[0, 1]], base=SPARE, channel_multiplier=1,
                           allow_small_or_imprecise_dtypes=True).then_inc(consts, 1)
            pool.wait_ge(consts, 4)
            nc.gpsimd.affine_select(out=ident[:, :], in_=ident[:, :], compare_op=ALU.not_equal, fill=1.0,
                                    base=0, pattern=[[-1, P]], channel_multiplier=1).then_inc(consts, 1)
            nc.gpsimd.affine_select(out=before[:, :], in_=before[:, :], compare_op=ALU.is_gt, fill=0.0,
                                    base=0, pattern=[[-1, P]], channel_multiplier=1).then_inc(consts, 1)
            pool.wait_ge(idx_loaded, 64)

            def gidx_copy(i):
                if not isinstance(i, int) or i > 0:
                    for k in range(T):
                        pool.wait_ge(gathered[k], 32 * i)
                nc.gpsimd.tensor_copy(gidx[:, 0, :], src_all[:, i, :])
                nc.gpsimd.tensor_copy(gidx[:, 1, :], dst_all[:, i, :]).then_inc(gidx_set, 1)
                pool.wait_ge(gidx_set, i + 1)

            def gather(i, k):
                wait(pool, normed[0], T * (i - 1) + k + 1 if not isinstance(i, int) or i > 0 else 0)
                pool.sem_inc(pool_passed, 1)
                for s in range(2):
                    nc.gpsimd.indirect_dma_start(
                        gath[:, s, k, :], None, x,
                        bass.IndirectOffsetOnAxis(ap=gidx[:, s, k:k + 1], axis=0)).then_inc(gathered[k], 16)

            def scatter(i, k):
                if k == 0:
                    pool.wait_ge(relsum_set, i + 1)
                    pool.wait_ge(sidx_set, i + 1)
                wait(pool, scattered, 16 * (T * i + k))
                pool.sem_inc(pool_passed, 1)
                nc.gpsimd.indirect_dma_start(
                    agg, bass.IndirectOffsetOnAxis(ap=sidx[:, k:k + 1], axis=0),
                    relsum[:, k, :], None, compute_op=ALU.add).then_inc(scattered, 16)

            for i in (0, 1):
                gidx_copy(i)
                for k in range(T):
                    gather(i, k)
            pool.wait_ge(zeroed, 32)

            def gather_and_scatter(i):
                gidx_copy(i + 1)
                for k in range(T):
                    gather(i + 1, k)
                    scatter(i - 1, k)

            gather_and_scatter(1)
            with pool.Fori(2, EG) as i:
                gather_and_scatter(i)
            for i in (EG - 1, EG):
                for k in range(T):
                    scatter(i, k)

            def keep_x(r, j, u):
                pool.wait_ge(x_loaded[r], 16 * (j + 1))
                pool.wait_ge(results, u - 1)
                nc.gpsimd.tensor_tensor(xb[r][:, :, :], xin[r][:, :, :],
                                        b2n[:, :].unsqueeze(1).to_broadcast([P, T, D]), ALU.add).then_inc(xb_set[r], 1)

            pool.wait_ge(loaded, LOADS)
            keep_x(1, 0, EG + 1)
            keep_x(2, 0, EG + 2)
            with pool.Fori(1, NP) as j:
                keep_x(1, j, EG + 1 + 2 * j)
                keep_x(2, j, EG + 2 + 2 * j)
            keep_x(1, NP, EG + 1 + 2 * NP)
            keep_x(2, NP, EG + 2 + 2 * NP)

        @block.tensor
        def _(pe):
            def transpose_edges(i):
                pe.wait_ge(ea_loaded, 16 * (i + 1))
                for k in range(T):
                    last = nc.tensor.transpose(tps[2][:, k * P:(k + 1) * P], ea_in[:, k, :], ident[:, :])
                last.then_inc(ea_used, 1)
                pe.wait_ge(dst_cast, i + 1)
                wait(pe, dup_set, i)
                for k in range(T):
                    last = nc.tensor.transpose(rowps[:, k * P:(k + 1) * P],
                                               dstf[:, k:k + 1].to_broadcast([P, P]), ident[:, :])
                for k in range(T):
                    pe.wait_ge(normed[0], T * i + k + 1)
                    for s in range(2):
                        last = nc.tensor.transpose(tps[s][:, k * P:(k + 1) * P], h[0][:, s * T + k, :], ident[:, :])
                last.then_inc(transposed[0], 1)

            def transpose_nodes(r, j):
                pe.wait_ge(agg_loaded[r], 16 * (j + 1))
                for k in range(T):
                    last = nc.tensor.transpose(tps[1][:, k * P:(k + 1) * P], agg_in[r][:, k, :], ident[:, :])
                last.then_inc(agg_used[r], 1)
                pe.wait_ge(normed[r], T * (j + 1))
                for k in range(T):
                    last = nc.tensor.transpose(tps[0][:, k * P:(k + 1) * P], h[r][:, k, :], ident[:, :])
                last.then_inc(transposed[r], 1)

            def layer1(r, n, u, c):
                if c == 0:
                    pe.wait_ge(inT_act[r], n + 1)
                    pe.wait_ge(inT_dve[r], n + 1)
                wait(pe, hid_set, C * (u - 1) + c + 1 if not isinstance(u, int) or u > 0 else 0)
                w = w1e if r == 0 else w1n
                K = w.shape[1]
                for q in range(K):
                    last = nc.tensor.matmul(l1ps[c][:, :], w[:, q, c * P:(c + 1) * P], inT[r][:, q, :],
                                            start=(q == 0), stop=(q == K - 1))
                last.then_inc(l1_done, 1)

            def layer2(r, u):
                pe.wait_ge(hid_set, C * (u + 1))
                wait(pe, results, u)
                w = w2e if r == 0 else w2n
                for k in range(T):
                    for c in range(C):
                        last = nc.tensor.matmul(l2ps[:, k * P:(k + 1) * P], hid[r][:, c, k * P:(k + 1) * P],
                                                w[:, c, :], start=(c == 0), stop=(c == C - 1))
                last.then_inc(l2_done, 1)

            def sum_same(i, u):
                pe.wait_ge(results, u + 1)
                wait(pe, relsum_set, i)
                for k in range(T):
                    last = nc.tensor.matmul(sumps[:, k * P:(k + 1) * P], same[:, k, :], rel[:, k, :],
                                            start=True, stop=True)
                last.then_inc(summed, 1)

            def edge_group(i):
                transpose_edges(i)
                layer1(0, i, i, 0)
                layer1(0, i, i, 1)
                layer2(0, i)
                sum_same(i, i)

            def node_pair(j, u):
                transpose_nodes(1, j)
                layer1(1, j, u, 0)
                transpose_nodes(2, j)
                layer1(1, j, u, 1)
                layer1(2, j, u + 1, 0)
                layer2(1, u)
                layer1(2, j, u + 1, 1)
                layer2(2, u + 1)

            pe.wait_ge(consts, 6)
            pe.wait_ge(loaded, LOADS)
            edge_group(0)
            with pe.Fori(1, EG + 1) as i:
                edge_group(i)
            node_pair(0, EG + 1)
            with pe.Fori(1, NP) as j:
                node_pair(j, EG + 1 + 2 * j)
            node_pair(NP, EG + 1 + 2 * NP)

        @block.scalar
        def _(act):
            act.wait_ge(zeros_set, 1)
            Q = zeros.shape[1]
            R = N * D // (P * Q)
            assert R * P * Q == N * D
            whole = agg[0:N, :].rearrange("n f -> (n f)").rearrange("(p r q) -> p r q", r=R, q=Q)
            act.dma_start(whole, zeros[:, :].unsqueeze(1).to_broadcast([P, R, Q])).then_inc(zeroed, 16)
            act.dma_start(agg[N:N + P, :], zeros[:, 0:D]).then_inc(zeroed, 16)

            def deviations(r, n):
                act.wait_ge(moments[r], n + 1)
                nc.scalar.activation(sd[r][:, :], mv[r][:, :, 1], ACT.Sqrt, bias=eps[:, 0:1]).then_inc(deviation[r], 1)

            def evacuate_edges(i):
                act.wait_ge(ea_used, i + 1)
                nc.scalar.activation(inT[0][:, 2, :], tps[2][:, :], ACT.Copy)
                act.wait_ge(transposed[0], i + 1)
                nc.scalar.activation(inT[0][:, 0, :], tps[0][:, :], ACT.Relu).then_inc(inT_act[0], 1)

            def evacuate_nodes(r, j):
                act.wait_ge(agg_used[r], j + 1)
                nc.scalar.activation(inT[r][:, 1, :], tps[1][:, :], ACT.Copy).then_inc(inT_act[r], 1)

            def hidden(r, u, c, prev):
                act.wait_ge(l1_done, C * u + c + 1)
                if c == 0:
                    wait(act, l2_done, prev)
                b = b1e if r == 0 else b1n
                nc.scalar.activation(hid[r][:, c, :], l1ps[c][:, :], ACT.Relu, bias=b[:, c:c + 1]).then_inc(hid_set, 1)

            def sums(i):
                act.wait_ge(summed, i + 1)
                wait(act, scattered, 16 * T * i)
                nc.scalar.activation(relsum[:, :, :], sumps[:, :].rearrange("p (k f) -> p k f", k=T),
                                     ACT.Copy).then_inc(relsum_set, 1)

            act.wait_ge(consts, 6)
            act.wait_ge(loaded, LOADS)

            def edge_group(i):
                deviations(0, i)
                evacuate_edges(i)
                hidden(0, i, 0, i)
                hidden(0, i, 1, i)
                sums(i)

            def node_pair(j, u):
                deviations(1, j)
                evacuate_nodes(1, j)
                deviations(2, j)
                hidden(1, u, 0, u - 1)
                evacuate_nodes(2, j)
                hidden(1, u, 1, u - 1)
                hidden(2, u + 1, 0, u)
                hidden(2, u + 1, 1, u)

            edge_group(0)
            with act.Fori(1, EG + 1) as i:
                edge_group(i)
            node_pair(0, EG + 1)
            with act.Fori(1, NP) as j:
                node_pair(j, EG + 1 + 2 * j)
            node_pair(NP, EG + 1 + 2 * NP)

            act.wait_ge(zeroed, 32)

        @block.vector
        def _(dve):
            def statistics(r, n, source):
                last = None
                for t in range(tiles[r]):
                    if r == 0 and t % 2 == 0:
                        dve.wait_ge(gathered[t // 2], 32 * (n + 1))
                    last = nc.vector.bn_stats(st[r][:, t, :], source(t))
                last.then_inc(stats[r], 1)
                dve.wait_ge(stats[r], n + 1)
                dve.sem_inc(dve_passed, 1)
                for t in range(tiles[r]):
                    last = nc.vector.bn_aggr(mv[r][:, t, :], st[r][:, t, :])
                last.then_inc(moments[r], 1)

            def normalise(r, n, source):
                dve.wait_ge(deviation[r], n + 1)
                nc.vector.reciprocal(rs[r][:, :], sd[r][:, :]).then_inc(inverse[r], 1)
                dve.wait_ge(inverse[r], n + 1)
                for t in range(tiles[r]):
                    last = nc.vector.tensor_scalar(h[r][:, where(r, t), :], source(t), mv[r][:, t, 0:1],
                                                   rs[r][:, t:t + 1], ALU.subtract, ALU.mult)
                    if r or t % 2:
                        last.then_inc(normed[r], 1)

            def where(r, t):
                return (t % 2) * T + t // 2 if r == 0 else t

            def edge_source(t):
                return gath[:, t % 2, t // 2, :]

            def node_source(r):
                return lambda t: xin[r][:, t, :]

            def edge_sameness(i):
                wait(dve, summed, i)
                for k in range(T):
                    nc.vector.tensor_scalar(same[:, k, :], rowps[:, k * P:(k + 1) * P], dstf[:, k:k + 1], None,
                                            ALU.is_equal)
                for k in range(T):
                    last = nc.vector.scalar_tensor_tensor(
                        out=junk[:, k, :], in0=rowps[:, k * P:(k + 1) * P], scalar=dstf[:, k:k + 1],
                        in1=before[:, :], op0=ALU.is_equal, op1=ALU.mult, accum_out=dup[:, k:k + 1])
                last.then_inc(dup_set, 1)
                dve.wait_ge(dup_set, i + 1)
                nc.vector.tensor_scalar(off[:, :], dstf[:, :], -1.0, spare[:, 0:1], ALU.mult, ALU.add)
                nc.vector.tensor_scalar(dups[:, :], dup[:, :], 1.0, None, ALU.min).then_inc(off_set, 1)
                dve.wait_ge(off_set, i + 1)
                nc.vector.tensor_tensor(off2[:, :], off[:, :], dups[:, :], ALU.mult).then_inc(off2_set, 1)
                dve.wait_ge(off2_set, i + 1)
                wait(dve, scattered, 16 * T * i)
                nc.vector.tensor_tensor(sidx[:, :], off2[:, :], dstf[:, :], ALU.add).then_inc(sidx_set, 1)

            def evacuate_edges(i):
                dve.wait_ge(transposed[0], i + 1)
                nc.vector.tensor_scalar(inT[0][:, 1, :], tps[1][:, :], 0.0, None, ALU.max).then_inc(inT_dve[0], 1)

            def evacuate_nodes(r, j):
                dve.wait_ge(transposed[r], j + 1)
                nc.vector.tensor_scalar(inT[r][:, 0, :], tps[0][:, :], 0.0, None, ALU.max).then_inc(inT_dve[r], 1)

            def edge_results(i, u):
                dve.wait_ge(l2_done, u + 1)
                wait(dve, summed, i)
                nc.vector.tensor_tensor(rel[:, :, :], l2ps[:, :].rearrange("p (k f) -> p k f", k=T),
                                        b2e[:, :].unsqueeze(1).to_broadcast([P, T, D]), ALU.add).then_inc(results, 1)

            def node_results(r, j, u):
                dve.wait_ge(l2_done, u + 1)
                dve.wait_ge(xb_set[r], j + 1)
                wait(dve, stored[r], 16 * j)
                nc.vector.tensor_tensor(res[r][:, :, :], l2ps[:, :].rearrange("p (k f) -> p k f", k=T),
                                        xb[r][:, :, :], ALU.add).then_inc(results, 1)

            dve.wait_ge(consts, 6)
            dve.wait_ge(idx_loaded, 64)
            dve.wait_ge(loaded, LOADS)

            def edge_group(i):
                if isinstance(i, int):
                    nc.vector.tensor_copy(dstf[:, :], dst_all[:, i, :]).then_inc(tail_cast, 1)
                    dve.wait_ge(tail_cast, 1)
                    nc.vector.tensor_copy(dstf[0:DONE, :], spare[0:DONE, 0:1].to_broadcast([DONE, T])).then_inc(dst_cast, 1)
                else:
                    wait(dve, dup_set, i)
                    wait(dve, sidx_set, i)
                    wait(dve, transposed[0], i)
                    nc.vector.tensor_copy(dstf[:, :], dst_all[:, i, :]).then_inc(dst_cast, 1)
                statistics(0, i, edge_source)
                normalise(0, i, edge_source)
                evacuate_edges(i)
                dve.wait_ge(dst_cast, i + 1)
                edge_sameness(i)
                edge_results(i, i)

            def node_pair(j, u):
                for r in (1, 2):
                    dve.wait_ge(x_loaded[r], 16 * (j + 1))
                    statistics(r, j, node_source(r))
                for r in (1, 2):
                    normalise(r, j, node_source(r))
                evacuate_nodes(1, j)
                evacuate_nodes(2, j)
                node_results(1, j, u)
                node_results(2, j, u + 1)

            edge_group(0)
            with dve.Fori(1, EG + 1) as i:
                edge_group(i)
            node_pair(0, EG + 1)
            with dve.Fori(1, NP) as j:
                node_pair(j, EG + 1 + 2 * j)
            node_pair(NP, EG + 1 + 2 * NP)


_INS = ["x", "src", "dst", "edge_attr_128", "L0_gnn_re_w1", "L0_gnn_re_b1", "L0_gnn_re_w2", "L0_gnn_re_b2",
        "L0_gnn_ea_w1", "L0_gnn_ea_b1", "L0_gnn_ea_w2", "L0_gnn_ea_b2"]


def kernel(**inputs):
    import numpy as np
    import concourse.bacc as bacc
    from concourse.bass_utils import run_bass_kernel_spmd

    nc = bacc.Bacc("TRN2", target_bir_lowering=False, num_devices=1)
    arrays, args = {}, []
    for name in _INS:
        a = np.ascontiguousarray(inputs[name])
        arrays[f"in_{name}"] = a
        args.append(nc.dram_tensor(f"in_{name}", a.shape, mybir.dt.from_np(a.dtype), kind="ExternalInput").ap())
    out = nc.dram_tensor("out", arrays["in_x"].shape, F32, kind="ExternalOutput").ap()
    gnn_program(nc, *args, out)
    r = run_bass_kernel_spmd(nc, [arrays], core_ids=[0])
    return r.results[0]["out"]
```

```python
import concourse.bass as bass
from concourse import mybir
from contextlib import ExitStack

P = 128
F32 = mybir.dt.float32
F32R = mybir.dt.float32r
I32 = mybir.dt.int32
ALU = mybir.AluOpType
ACT = mybir.ActivationFunctionType
AX = mybir.AxisListType


def gnn_program(nc, x, src, dst, ea, re_w1, re_b1, re_w2, re_b2, ea_w1, ea_b1, ea_w2, ea_b2, out):
    N, D = x.shape
    E = src.shape[0]
    HID = re_w1.shape[1]
    C = HID // P
    T = 4
    G = T * P
    EG = E // G
    EDGE_TAIL = E - G
    DONE = (EG * G - EDGE_TAIL) // T
    NP = N // (2 * G)
    NODE_TAIL = N - 2 * G
    SPARE = N
    EPS = 1e-5
    LOADS = 16 * (4 + 2 * C + 2)
    LAG = 3
    FIRST = 4
    MOST = EG - 4
    LOW = 8192
    assert (EG * G - EDGE_TAIL) % T == 0 and D == P and EG * G < E and NP * 2 * G < N and NP == EG
    assert FIRST > LAG

    agg = nc.dram_tensor("agg", [N + P, D], F32, kind="Internal").ap()

    ctx = ExitStack()
    with ctx:
        def sb(name, shape, dt=F32):
            return ctx.enter_context(nc.sbuf_tensor(name, shape, dt))

        def ps(name, shape):
            return ctx.enter_context(nc.psum_tensor(name, shape, F32))

        def sem(name):
            return ctx.enter_context(nc.semaphore(name))

        w1 = [sb("w1e", [P, 3, HID]), sb("w1n", [P, 2, HID])]
        w1hi = [sb("w1e_hi", [P, 3, HID], F32R), sb("w1n_hi", [P, 2, HID], F32R)]
        w1lo = [sb("w1e_lo", [P, 3, HID], F32R), sb("w1n_lo", [P, 2, HID], F32R)]
        w2 = [sb("w2e", [P, C, D]), sb("w2n", [P, C, D])]
        b1 = [sb("b1e", [P, C]), sb("b1n", [P, C])]
        b2e = sb("b2e", [P, D])
        b2n = sb("b2n", [P, D])
        ident = sb("ident", [P, P])
        rank_bits = sb("rank_bits", [P, 2], I32)
        rank_f = sb("rank_f", [P, 2], I32)
        rank = sb("rank", [P, 2], F32R)
        rank2 = sb("rank2", [P, 1])
        spare = sb("spare", [P, 1])
        eps = sb("eps", [P, 1])
        ZQ = 2621
        zeros = sb("zeros", [P, ZQ])
        dst_rows = sb("dst_rows", [EG + 1, G], I32)
        least = sb("least", [EG + 1, 1], I32)
        least_pair = sb("least_pair", [EG + 1, 1], I32)
        group_no = sb("group_no", [EG + 1, 1])
        need = sb("need", [EG + 1, 2])
        plan = sb("plan", [1, 8])
        ctrl = sb("ctrl", [1, 4 + FIRST], I32)
        src_all = sb("src_all", [P, EG + 1, T], I32)
        dst_all = sb("dst_all", [P, EG + 1, T], I32)
        gidx = sb("gidx", [P, 2, T], I32)
        sidx_new = sb("sidx_new", [P, T], I32)
        sidx = sb("sidx", [P, T], I32)
        gath = sb("gath", [P, 2, T, D])
        ea_in = sb("ea_in", [P, T, D])
        dstf = sb("dstf", [P, T])
        same = sb("same", [P, T, P], F32R)
        off = sb("off", [P, T])
        off2 = sb("off2", [P, T])
        rel = sb("rel", [P, G])
        rel_hi = sb("rel_hi", [P, G], F32R)
        rel_lo = sb("rel_lo", [P, G], F32R)
        relsum = [sb(f"relsum{b}", [P, T, D]) for b in range(2)]
        tiles = [2 * T, T, T]
        parts = [3, 2, 2]
        h = [sb(f"h{r}", [P, tiles[r], D]) for r in range(3)]
        st = [sb(f"st{r}", [P, tiles[r], 6]) for r in range(3)]
        mv = [sb(f"mv{r}", [P, tiles[r], 2]) for r in range(3)]
        sd = [sb(f"sd{r}", [P, tiles[r]]) for r in range(3)]
        rs = [sb(f"rs{r}", [P, tiles[r]]) for r in range(3)]
        shift = [None] + [sb(f"shift{r}", [P, T]) for r in (1, 2)]
        hi = [sb(f"hi{r}", [P, parts[r], G], F32R) for r in range(3)]
        lo = [sb(f"lo{r}", [P, parts[r], G], F32R) for r in range(3)]
        hid = [sb(f"hid{r}", [P, C, G]) for r in range(3)]
        xin = [None] + [sb(f"xin{r}", [P, T, D]) for r in (1, 2)]
        xb = [None] + [sb(f"xb{r}", [P, T, D]) for r in (1, 2)]
        agg_in = [None] + [sb(f"agg_in{r}", [P, T, D]) for r in (1, 2)]
        res = [None] + [sb(f"res{r}", [P, T, D]) for r in (1, 2)]

        tps = [ps(f"tps{b}", [P, G]) for b in range(3)]
        rowps = ps("rowps", [P, G])
        l1ps = [ps(f"l1ps{c}", [P, G]) for c in range(C)]
        l2ps = ps("l2ps", [P, G])
        sumps = ps("sumps", [P, G])

        loaded = sem("loaded")
        first_idx = sem("first_idx")
        idx_loaded = sem("idx_loaded")
        rows_loaded = sem("rows_loaded")
        consts = sem("consts")
        low_zeroed = sem("low_zeroed")
        zeroed = sem("zeroed")
        zeros_set = sem("zeros_set")
        split = sem("split")
        ranked = sem("ranked")
        planning = sem("planning")
        need_set = sem("need_set")
        need_turned = sem("need_turned")
        ctrl_set = sem("ctrl_set")
        gidx_set = sem("gidx_set")
        gathered = [sem(f"gathered{k}") for k in range(T)]
        ea_loaded = sem("ea_loaded")
        ea_used = sem("ea_used")
        scattered = sem("scattered")
        tail_cast = sem("tail_cast")
        dst_cast = sem("dst_cast")
        same_set = sem("same_set")
        counted = sem("counted")
        off_set = sem("off_set")
        off2_set = sem("off2_set")
        sidx_set = sem("sidx_set")
        sidx_kept = sem("sidx_kept")
        rows_turned = sem("rows_turned")
        rel_set = sem("rel_set")
        relhi_set = sem("relhi_set")
        summed = sem("summed")
        relsum_set = sem("relsum_set")
        stats = [sem(f"stats{r}") for r in range(3)]
        moments = [sem(f"moments{r}") for r in range(3)]
        deviation = [sem(f"deviation{r}") for r in range(3)]
        inverse = [sem(f"inverse{r}") for r in range(3)]
        shift_set = [None] + [sem(f"shift_set{r}") for r in (1, 2)]
        normed = [sem(f"normed{r}") for r in range(3)]
        transposed = [sem(f"transposed{r}") for r in range(3)]
        hi_set = [sem(f"hi_set{r}") for r in range(3)]
        lo_set = [sem(f"lo_set{r}") for r in range(3)]
        x_loaded = [None] + [sem(f"x_loaded{r}") for r in (1, 2)]
        xb_set = [None] + [sem(f"xb_set{r}") for r in (1, 2)]
        agg_loaded = [None] + [sem(f"agg_loaded{r}") for r in (1, 2)]
        agg_used = [None] + [sem(f"agg_used{r}") for r in (1, 2)]
        stored = [None] + [sem(f"stored{r}") for r in (1, 2)]
        l1_done = sem("l1_done")
        hid_set = sem("hid_set")
        l2_done = sem("l2_done")
        results = sem("results")
        pool_passed = sem("pool_passed")
        dve_passed = sem("dve_passed")

        def rows(t, start):
            return t[bass.ds(start, G), :].rearrange("(p k) f -> p k f", k=T)

        def tiled(t):
            return t[:, :].rearrange("p (k f) -> p k f", k=T)

        def wait(eng, s, value):
            if not isinstance(value, int) or value > 0:
                eng.wait_ge(s, value)

        def read_plan(eng):
            eng.wait_ge(ctrl_set, 1)
            lead = FIRST + eng.value_load(ctrl[0:1, 0:1], min_val=0, max_val=EG + 1 - FIRST)
            bound = FIRST + eng.value_load(ctrl[0:1, 1:2], min_val=0, max_val=EG - 1 - FIRST)
            alone = 1 + eng.value_load(ctrl[0:1, 2:3], min_val=0, max_val=EG - FIRST)
            joint = eng.value_load(ctrl[0:1, 3:4], min_val=0, max_val=EG - 1 - FIRST)
            return eng.snap(lead), eng.snap(bound), eng.snap(alone), joint

        def run(eng, edge_step, enter, step, pair_step, pairs_enter=None, finish_edges=None):
            for e in range(FIRST):
                edge_step(e)
            lead, bound, alone, joint = read_plan(eng)
            with eng.If(lead > FIRST):
                with eng.Fori(FIRST, bound) as e:
                    edge_step(e)
            with eng.If(lead < EG + 1):
                few = lead.with_bounds(min_val=FIRST, max_val=MOST)
                enter(few)
                step(few, 0, 0)
                with eng.Fori(1, joint) as j:
                    step((few + j).with_bounds(min_val=FIRST + 1, max_val=EG - 2), j, 0)
                step(EG - 1, joint, 1)
                step(EG, joint + 1, 2)
            with eng.Else():
                edge_step(EG - 1)
                edge_step(EG)
                if finish_edges:
                    finish_edges()
                pair_step(0, 0)
            if pairs_enter:
                pairs_enter()
            pair_step(alone, 3)
            with eng.Fori(alone + 1, NP - 1) as j:
                pair_step(j, 0)
            pair_step(NP - 1, 1)
            pair_step(NP, 2)

        def early(e):
            return isinstance(e, int) and e < FIRST

        def sum_buffer(e):
            return (FIRST - 1 - e) % 2 if early(e) else 0

        def turn_alone(j):
            return EG + 1 + 2 * j

        block = ctx.enter_context(nc.Block())

        @block.sync
        def _(sp):
            for side, t in ((src, src_all), (dst, dst_all)):
                whole = side[0:EG * G].rearrange("(g p k) -> p g k", p=P, k=T)
                sp.dma_start(t[:, 0:2, :], whole[:, 0:2, :]).then_inc(first_idx, 16)
            for side, t in ((src, src_all), (dst, dst_all)):
                whole = side[0:EG * G].rearrange("(g p k) -> p g k", p=P, k=T)
                sp.dma_start(t[:, 2:EG, :], whole[:, 2:EG, :]).then_inc(idx_loaded, 16)
                sp.dma_start(t[:, EG, :], side[EDGE_TAIL:E].rearrange("(p k) -> p k", k=T)).then_inc(idx_loaded, 16)
            for t, w in ((w1[0], re_w1), (w2[0], re_w2), (w1[1], ea_w1), (w2[1], ea_w2)):
                sp.dma_start(t[:, :, :], w.rearrange("(c p) n -> p c n", p=P)).then_inc(loaded, 16)
            for t, b in ((b1[0], re_b1), (b1[1], ea_b1)):
                for c in range(C):
                    sp.dma_start(t[:, c:c + 1], b[c * P:(c + 1) * P].unsqueeze(1)).then_inc(loaded, 16)
            for t, b in ((b2e, re_b2), (b2n, ea_b2)):
                sp.dma_start(t[:, :], b.rearrange("(a n) -> a n", a=1).to_broadcast([P, D])).then_inc(loaded, 16)
            sp.dma_start(dst_rows[0:EG, :], dst[0:EG * G].rearrange("(g n) -> g n", n=G)).then_inc(rows_loaded, 16)
            sp.dma_start(dst_rows[EG:EG + 1, :], dst[EDGE_TAIL:E].unsqueeze(0)).then_inc(rows_loaded, 16)

            def load_ea(e, start):
                wait(sp, ea_used, e)
                sp.dma_start(ea_in[:, :, :], rows(ea, start)).then_inc(ea_loaded, 16)

            def load_x(j, start):
                for r in (1, 2):
                    wait(sp, normed[r], j * T)
                    wait(sp, xb_set[r], j)
                    sp.dma_start(xin[r][:, :, :], rows(x, start + (r - 1) * G)).then_inc(x_loaded[r], 16)

            def load_agg(j, start, edges):
                for r in (1, 2):
                    wait(sp, scattered, 16 * T * edges)
                    wait(sp, agg_used[r], j)
                    sp.dma_start(agg_in[r][:, :, :], rows(agg, start + (r - 1) * G)).then_inc(agg_loaded[r], 16)

            def store_nodes(start, turn, overlapped=0):
                for r in (1, 2):
                    sp.wait_ge(results, turn + r)
                    for other in (1, 2) if overlapped else ():
                        sp.wait_ge(stored[other], 16 * overlapped)
                    sp.dma_start(rows(out, start + (r - 1) * G), res[r][:, :, :]).then_inc(stored[r], 16)

            load_ea(0, 0)
            load_x(0, 0)

            def edge_step(e):
                if isinstance(e, int) and e == EG:
                    return
                tail = isinstance(e, int) and e == EG - 1
                load_ea(e + 1, EDGE_TAIL if tail else (e + 1) * G)

            def enter(lead):
                load_agg(0, 0, lead - LAG + 1)

            def step(e, j, kind):
                if kind < 2:
                    load_ea(e + 1, EDGE_TAIL if kind else (e + 1) * G)
                load_x(j + 1, (j + 1) * 2 * G)
                load_agg(j + 1, (j + 1) * 2 * G, e + 2 - LAG)
                store_nodes(j * 2 * G, e + 1 + 2 * j)

            def finish_edges():
                load_agg(0, 0, EG + 1)

            def pair_step(j, kind):
                if kind < 2 or kind == 3:
                    start = NODE_TAIL if kind == 1 else (j + 1) * 2 * G
                    load_x(j + 1, start)
                    load_agg(j + 1, start, EG if kind == 3 else EG + 1)
                    store_nodes(j * 2 * G, turn_alone(j))
                else:
                    store_nodes(NODE_TAIL, turn_alone(j), NP)

            run(sp, edge_step, enter, step, pair_step, finish_edges=finish_edges)
            for r in (1, 2):
                sp.wait_ge(stored[r], 16 * (NP + 1))

        @block.gpsimd
        def _(pool):
            pool.sem_inc(zeroed, 1)
            nc.gpsimd.memset(zeros[:, :], 0.0).then_inc(zeros_set, 1)
            pool.wait_ge(first_idx, 32)

            def copy_gidx(e):
                if not isinstance(e, int) or e > 0:
                    for k in range(T):
                        pool.wait_ge(gathered[k], 32 * e)
                pool.sem_inc(pool_passed, 1)
                nc.gpsimd.tensor_copy(gidx[:, 0, :], src_all[:, e, :])
                nc.gpsimd.tensor_copy(gidx[:, 1, :], dst_all[:, e, :]).then_inc(gidx_set, 1)
                pool.wait_ge(gidx_set, e + 1)

            def gather(e, k):
                if not isinstance(e, int) or e > 0:
                    pool.wait_ge(normed[0], T * (e - 1) + k + 1)
                pool.sem_inc(pool_passed, 1)
                for s in range(2):
                    nc.gpsimd.indirect_dma_start(
                        gath[:, s, k, :], None, x,
                        bass.IndirectOffsetOnAxis(ap=gidx[:, s, k:k + 1], axis=0)).then_inc(gathered[k], 16)

            def scatter(e, k):
                if k == 0:
                    pool.wait_ge(relsum_set, e + 1)
                    pool.wait_ge(sidx_set, e + 1)
                    wait(pool, scattered, 16 * T * e)
                    pool.sem_inc(pool_passed, 1)
                    nc.gpsimd.tensor_copy(sidx[:, :], sidx_new[:, :]).then_inc(sidx_kept, 1)
                    pool.wait_ge(sidx_kept, e + 1)
                    if isinstance(e, int) and e < FIRST:
                        flag = pool.value_load(ctrl[0:1, 4 + e:5 + e], min_val=1, max_val=17)
                        pool.wait_ge(low_zeroed, 32)
                        pool.wait_ge(zeroed, flag)
                wait(pool, scattered, 16 * (T * e + k))
                pool.sem_inc(pool_passed, 1)
                nc.gpsimd.indirect_dma_start(
                    agg, bass.IndirectOffsetOnAxis(ap=sidx[:, k:k + 1], axis=0),
                    relsum[sum_buffer(e)][:, k, :], None, compute_op=ALU.add).then_inc(scattered, 16)

            def keep_x(r, j, before):
                pool.wait_ge(x_loaded[r], 16 * (j + 1))
                pool.wait_ge(results, before)
                nc.gpsimd.tensor_tensor(xb[r][:, :, :], xin[r][:, :, :],
                                        b2n[:, :].unsqueeze(1).to_broadcast([P, T, D]), ALU.add).then_inc(xb_set[r], 1)

            copy_gidx(0)
            for k in range(T):
                gather(0, k)
            nc.gpsimd.memset(ident[:, :], 0.0).then_inc(consts, 1)
            nc.gpsimd.memset(eps[:, :], EPS).then_inc(consts, 1)
            nc.gpsimd.iota(spare[:, :], pattern=[[0, 1]], base=SPARE, channel_multiplier=1,
                           allow_small_or_imprecise_dtypes=True).then_inc(consts, 1)
            nc.gpsimd.iota(group_no[:, :], pattern=[[0, 1]], base=0, channel_multiplier=1,
                           allow_small_or_imprecise_dtypes=True).then_inc(consts, 1)
            nc.gpsimd.iota(rank_bits[:, :], pattern=[[0, 2]], base=444, channel_multiplier=-3).then_inc(consts, 1)
            pool.wait_ge(consts, 5)
            nc.gpsimd.affine_select(out=ident[:, :], in_=ident[:, :], compare_op=ALU.not_equal, fill=1.0,
                                    base=0, pattern=[[-1, P]], channel_multiplier=1).then_inc(consts, 1)
            copy_gidx(1)
            for k in range(T):
                gather(1, k)
            pool.wait_ge(idx_loaded, 64)
            pool.wait_ge(ctrl_set, 1)

            def edge_step(e, joint=False):
                more = not isinstance(e, int) or e + 2 <= EG
                mixed = joint or early(e)
                if more and mixed:
                    copy_gidx(e + 2)
                for k in range(T):
                    if not isinstance(e, int) or e > 0:
                        scatter(e - 1, k)
                    if more and mixed:
                        gather(e + 2, k)
                if more and not mixed:
                    copy_gidx(e + 2)
                    for k in range(T):
                        gather(e + 2, k)
                if isinstance(e, int) and e == EG:
                    for k in range(T):
                        scatter(e, k)
                if isinstance(e, int) and e == FIRST - 1:
                    pool.wait_ge(low_zeroed, 32)
                    pool.wait_ge(zeroed, 17)

            def step(e, j, kind):
                pool.wait_ge(loaded, LOADS)
                keep_x(1, j, e + 2 * j - 1)
                keep_x(2, j, e + 2 * j)
                edge_step(e, joint=True)

            def pair_step(j, kind):
                pool.wait_ge(loaded, LOADS)
                keep_x(1, j, turn_alone(j) - 1)
                keep_x(2, j, turn_alone(j))

            run(pool, edge_step, lambda lead: None, step, pair_step)

        @block.tensor
        def _(pe):
            def transpose_edges(e):
                pe.wait_ge(ea_loaded, 16 * (e + 1))
                for k in range(T):
                    last = nc.tensor.transpose(tps[2][:, k * P:(k + 1) * P], ea_in[:, k, :], ident[:, :])
                last.then_inc(ea_used, 1)
                for k in range(T):
                    pe.wait_ge(normed[0], T * e + k + 1)
                    for s in range(2):
                        last = nc.tensor.transpose(tps[s][:, k * P:(k + 1) * P], h[0][:, s * T + k, :], ident[:, :])
                last.then_inc(transposed[0], 1)
                pe.wait_ge(dst_cast, e + 1)
                wait(pe, off2_set, e)
                for k in range(T):
                    last = nc.tensor.transpose(rowps[:, k * P:(k + 1) * P],
                                               dstf[:, k:k + 1].to_broadcast([P, P]), ident[:, :])
                last.then_inc(rows_turned, 1)

            def transpose_nodes(r, j):
                pe.wait_ge(agg_loaded[r], 16 * (j + 1))
                for k in range(T):
                    last = nc.tensor.transpose(tps[1][:, k * P:(k + 1) * P], agg_in[r][:, k, :], ident[:, :])
                last.then_inc(agg_used[r], 1)
                pe.wait_ge(normed[r], T * (j + 1))
                for k in range(T):
                    last = nc.tensor.transpose(tps[0][:, k * P:(k + 1) * P], h[r][:, k, :], ident[:, :])
                last.then_inc(transposed[r], 1)

            def layer1(r, n, turn, c):
                K = parts[r]
                w = min(r, 1)
                wait(pe, hid_set, C * (turn - 1) + c + 1 if not isinstance(turn, int) or turn > 0 else 0)
                if c == 0:
                    pe.wait_ge(hi_set[r], K * (n + 1))
                for q in range(K):
                    for part, first in ((w1hi[w], True), (w1lo[w], False)):
                        nc.tensor.matmul(l1ps[c][:, :], part[:, q, c * P:(c + 1) * P], hi[r][:, q, :],
                                         start=(q == 0 and first), stop=False)
                if c == 0:
                    pe.wait_ge(lo_set[r], n + 1)
                for q in range(K):
                    last = nc.tensor.matmul(l1ps[c][:, :], w1hi[w][:, q, c * P:(c + 1) * P], lo[r][:, q, :],
                                            start=False, stop=(q == K - 1))
                last.then_inc(l1_done, 1)

            def layer2(r, turn):
                pe.wait_ge(hid_set, C * (turn + 1))
                wait(pe, results, turn)
                w = w2[min(r, 1)]
                for k in range(T):
                    for c in range(C):
                        last = nc.tensor.matmul(l2ps[:, k * P:(k + 1) * P], hid[r][:, c, k * P:(k + 1) * P],
                                                w[:, c, :], start=(c == 0), stop=(c == C - 1))
                last.then_inc(l2_done, 1)

            def count_same(e):
                pe.wait_ge(same_set, e + 1)
                for k in range(T):
                    last = nc.tensor.matmul(rowps[:, 2 * k:2 * k + 2], same[:, k, :], rank[:, :],
                                            start=True, stop=True)
                last.then_inc(counted, 1)

            def sum_same(e, turn):
                pe.wait_ge(results, turn + 1)
                wait(pe, relsum_set, e)
                for k in range(T):
                    for part in (rel_hi, rel_lo):
                        last = nc.tensor.matmul(sumps[:, k * P:(k + 1) * P], same[:, k, :], part[:, k * P:(k + 1) * P],
                                                start=(part is rel_hi), stop=(part is rel_lo))
                last.then_inc(summed, 1)

            def edge_step(e):
                transpose_edges(e)
                layer1(0, e, e, 0)
                layer1(0, e, e, 1)
                count_same(e)
                layer2(0, e)
                sum_same(e, e)

            def step(e, j, kind):
                turn = e + 2 * j
                layer1(0, e, turn, 0)
                transpose_nodes(1, j)
                layer1(0, e, turn, 1)
                layer1(1, j, turn + 1, 0)
                transpose_nodes(2, j)
                layer1(1, j, turn + 1, 1)
                count_same(e)
                layer2(0, turn)
                layer1(2, j, turn + 2, 0)
                if kind < 2:
                    transpose_edges(e + 1)
                layer1(2, j, turn + 2, 1)
                layer2(1, turn + 1)
                sum_same(e, turn)
                layer2(2, turn + 2)

            def pair_step(j, kind):
                turn = turn_alone(j)
                transpose_nodes(1, j)
                layer1(1, j, turn, 0)
                transpose_nodes(2, j)
                layer1(1, j, turn, 1)
                layer1(2, j, turn + 1, 0)
                layer2(1, turn)
                layer1(2, j, turn + 1, 1)
                layer2(2, turn + 1)

            pe.wait_ge(consts, 6)
            pe.wait_ge(need_set, 1)
            nc.tensor.transpose(sumps[0:1, 0:EG + 1], need[:, 0:1], ident[0:EG + 1, 0:EG + 1])
            nc.tensor.transpose(sumps[0:1, P:P + EG + 1], need[:, 1:2], ident[0:EG + 1, 0:EG + 1]).then_inc(need_turned, 1)
            pe.wait_ge(loaded, LOADS)
            pe.wait_ge(split, 1)
            pe.wait_ge(ranked, 1)
            run(pe, edge_step, transpose_edges, step, pair_step)

        @block.scalar
        def _(act):
            act.wait_ge(zeros_set, 1)

            def zero(start, end, to):
                n = (end - start) * D // P
                q = next(q for q in range(ZQ, 0, -1) if n % q == 0)
                flat = agg[start:end, :].rearrange("n f -> (n f)").rearrange("(p r q) -> p r q", r=n // q, q=q)
                act.dma_start(flat, zeros[:, 0:q].unsqueeze(1).to_broadcast([P, n // q, q])).then_inc(to, 16)

            def deviations(r, n):
                act.wait_ge(moments[r], n + 1)
                nc.scalar.activation(sd[r][:, :], mv[r][:, :, 1], ACT.Sqrt, bias=eps[:, 0:1]).then_inc(deviation[r], 1)

            def high_edges(e):
                act.wait_ge(ea_used, e + 1)
                nc.scalar.activation(hi[0][:, 2, :], tps[2][:, :], ACT.Copy).then_inc(hi_set[0], 1)
                act.wait_ge(transposed[0], e + 1)
                for q in range(2):
                    nc.scalar.activation(hi[0][:, q, :], tps[q][:, :], ACT.Relu).then_inc(hi_set[0], 1)

            def high_nodes(r, j):
                act.wait_ge(agg_used[r], j + 1)
                nc.scalar.activation(hi[r][:, 1, :], tps[1][:, :], ACT.Copy).then_inc(hi_set[r], 1)
                act.wait_ge(transposed[r], j + 1)
                nc.scalar.activation(hi[r][:, 0, :], tps[0][:, :], ACT.Relu).then_inc(hi_set[r], 1)

            def hidden(r, turn, c, before):
                act.wait_ge(l1_done, C * turn + c + 1)
                if c == 0:
                    wait(act, l2_done, before)
                b = b1[min(r, 1)]
                nc.scalar.activation(hid[r][:, c, :], l1ps[c][:, :], ACT.Relu, bias=b[:, c:c + 1]).then_inc(hid_set, 1)

            def normalise(r, j):
                act.wait_ge(shift_set[r], j + 1)
                for k in range(T):
                    last = nc.scalar.activation(h[r][:, k, :], xin[r][:, k, :], ACT.Identity,
                                                bias=shift[r][:, k:k + 1], scale=rs[r][:, k:k + 1])
                last.then_inc(normed[r], T)

            def high_rel(e):
                act.wait_ge(rel_set, e + 1)
                wait(act, summed, e)
                nc.scalar.activation(rel_hi[:, :], rel[:, :], ACT.Copy).then_inc(relhi_set, 1)

            def sums(e):
                act.wait_ge(summed, e + 1)
                wait(act, scattered, 16 * T * (max(e - 1, 0) if early(e) else e))
                nc.scalar.activation(relsum[sum_buffer(e)][:, :, :], tiled(sumps), ACT.Copy).then_inc(relsum_set, 1)

            act.wait_ge(consts, 6)
            act.wait_ge(loaded, LOADS)
            zero(0, LOW, low_zeroed)
            zero(SPARE, N + P, low_zeroed)
            zero(LOW, N, zeroed)

            def edge_step(e):
                deviations(0, e)
                high_edges(e)
                hidden(0, e, 0, e)
                hidden(0, e, 1, e)
                high_rel(e)
                sums(e)

            def enter(lead):
                deviations(0, lead)
                high_edges(lead)
                for r in (1, 2):
                    deviations(r, 0)
                for r in (1, 2):
                    normalise(r, 0)

            def enter_alone():
                for r in (1, 2):
                    deviations(r, 0)
                for r in (1, 2):
                    normalise(r, 0)

            def step(e, j, kind):
                turn = e + 2 * j
                hidden(0, turn, 0, turn)
                high_nodes(1, j)
                if kind < 2:
                    deviations(0, e + 1)
                hidden(0, turn, 1, turn)
                hidden(1, turn + 1, 0, turn)
                high_nodes(2, j)
                hidden(1, turn + 1, 1, turn)
                high_rel(e)
                hidden(2, turn + 2, 0, turn)
                if kind < 2:
                    high_edges(e + 1)
                deviations(1, j + 1)
                deviations(2, j + 1)
                hidden(2, turn + 2, 1, turn)
                normalise(1, j + 1)
                sums(e)
                normalise(2, j + 1)

            def pair_step(j, kind):
                turn = turn_alone(j)
                high_nodes(1, j)
                hidden(1, turn, 0, turn - 1)
                high_nodes(2, j)
                hidden(1, turn, 1, turn - 1)
                hidden(2, turn + 1, 0, turn)
                if kind != 2:
                    deviations(1, j + 1)
                    deviations(2, j + 1)
                hidden(2, turn + 1, 1, turn)
                if kind != 2:
                    normalise(1, j + 1)
                    normalise(2, j + 1)

            run(act, edge_step, enter, step, pair_step, finish_edges=enter_alone)
            act.wait_ge(low_zeroed, 32)
            act.wait_ge(zeroed, 17)

        @block.vector
        def _(dve):
            def statistics(r, n):
                for t in range(tiles[r]):
                    if r == 0 and t % 2 == 0:
                        dve.wait_ge(gathered[t // 2], 32 * (n + 1))
                    if r and t == 0:
                        dve.wait_ge(x_loaded[r], 16 * (n + 1))
                    last = nc.vector.bn_stats(st[r][:, t, :], source(r, t))
                last.then_inc(stats[r], 1)

            def combine(r, n):
                dve.wait_ge(stats[r], n + 1)
                dve.sem_inc(dve_passed, 1)
                for t in range(tiles[r]):
                    last = nc.vector.bn_aggr(mv[r][:, t, :], st[r][:, t, :])
                last.then_inc(moments[r], 1)

            def source(r, t):
                return xin[r][:, t, :] if r else gath[:, t % 2, t // 2, :]

            def invert(r, n):
                dve.wait_ge(deviation[r], n + 1)
                nc.vector.reciprocal(rs[r][:, :], sd[r][:, :]).then_inc(inverse[r], 1)

            def normalise_edges(e):
                dve.wait_ge(inverse[0], e + 1)
                for t in range(2 * T):
                    last = nc.vector.tensor_scalar(h[0][:, (t % 2) * T + t // 2, :], source(0, t), mv[0][:, t, 0:1],
                                                   rs[0][:, t:t + 1], ALU.subtract, ALU.mult)
                    if t % 2:
                        last.then_inc(normed[0], 1)

            def shifts(r, j):
                dve.wait_ge(inverse[r], j + 1)
                nc.vector.scalar_tensor_tensor(out=shift[r][:, :], in0=mv[r][:, :, 0], scalar=-1.0, in1=rs[r][:, :],
                                               op0=ALU.mult, op1=ALU.mult).then_inc(shift_set[r], 1)

            def cast_dst(e, tail=False):
                if not isinstance(e, int) or e > 0:
                    dve.wait_ge(rows_turned, e)
                    dve.wait_ge(sidx_set, e)
                if tail:
                    nc.vector.tensor_copy(dstf[:, :], dst_all[:, e, :]).then_inc(tail_cast, 1)
                    dve.wait_ge(tail_cast, 1)
                    nc.vector.tensor_copy(dstf[0:DONE, :], spare[0:DONE, 0:1].to_broadcast([DONE, T])).then_inc(dst_cast, 1)
                else:
                    nc.vector.tensor_copy(dstf[:, :], dst_all[:, e, :]).then_inc(dst_cast, 1)

            def mark_same(e):
                dve.wait_ge(rows_turned, e + 1)
                wait(dve, summed, e)
                nc.vector.tensor_tensor(same[:, :, :], tiled(rowps),
                                        dstf[:, :].unsqueeze(2).to_broadcast([P, T, P]), ALU.is_equal).then_inc(same_set, 1)

            def rows_to_add(e):
                dve.wait_ge(dst_cast, e + 1)
                nc.vector.tensor_scalar(off[:, :], dstf[:, :], -1.0, spare[:, 0:1], ALU.mult, ALU.add).then_inc(off_set, 1)
                dve.wait_ge(off_set, e + 1)
                dve.wait_ge(counted, e + 1)
                nc.vector.scalar_tensor_tensor(out=off2[:, :], in0=rowps[:, 0:2 * T].rearrange("p (k b) -> p k b", b=2)[:, :, 0],
                                               scalar=rank2[:, 0:1], in1=off[:, :],
                                               op0=ALU.is_ge, op1=ALU.mult).then_inc(off2_set, 1)
                dve.wait_ge(off2_set, e + 1)
                wait(dve, sidx_kept, e)
                nc.vector.tensor_tensor(sidx_new[:, :], off2[:, :], dstf[:, :], ALU.add).then_inc(sidx_set, 1)

            def low_edges(e):
                for n, q in enumerate((2, 0, 1)):
                    dve.wait_ge(hi_set[0], 3 * e + n + 1)
                    if q == 2:
                        nc.vector.tensor_tensor(lo[0][:, q, :], tps[q][:, :], hi[0][:, q, :].bitcast(F32), ALU.subtract)
                    else:
                        last = nc.vector.scalar_tensor_tensor(out=lo[0][:, q, :], in0=tps[q][:, :], scalar=0.0,
                                                              in1=hi[0][:, q, :].bitcast(F32), op0=ALU.max, op1=ALU.subtract)
                last.then_inc(lo_set[0], 1)

            def low_nodes(r, j):
                dve.wait_ge(hi_set[r], 2 * j + 1)
                nc.vector.tensor_tensor(lo[r][:, 1, :], tps[1][:, :], hi[r][:, 1, :].bitcast(F32), ALU.subtract)
                dve.wait_ge(hi_set[r], 2 * j + 2)
                nc.vector.scalar_tensor_tensor(out=lo[r][:, 0, :], in0=tps[0][:, :], scalar=0.0,
                                               in1=hi[r][:, 0, :].bitcast(F32), op0=ALU.max, op1=ALU.subtract).then_inc(lo_set[r], 1)

            def edge_results(e, turn):
                dve.wait_ge(l2_done, turn + 1)
                wait(dve, relhi_set, e)
                nc.vector.tensor_tensor(tiled(rel), tiled(l2ps),
                                        b2e[:, :].unsqueeze(1).to_broadcast([P, T, D]), ALU.add).then_inc(rel_set, 1)

            def low_rel(e, turn):
                dve.wait_ge(relhi_set, e + 1)
                wait(dve, summed, e)
                nc.vector.tensor_tensor(rel_lo[:, :], rel[:, :], rel_hi[:, :].bitcast(F32), ALU.subtract).then_inc(results, 1)

            def node_results(r, j, turn):
                dve.wait_ge(l2_done, turn + 1)
                dve.wait_ge(xb_set[r], j + 1)
                wait(dve, stored[r], 16 * j)
                nc.vector.tensor_tensor(res[r][:, :, :], tiled(l2ps), xb[r][:, :, :], ALU.add).then_inc(results, 1)

            steps = [0]

            def planned(ins):
                steps[0] += 1
                ins.then_inc(planning, 1)
                dve.wait_ge(planning, steps[0])

            dve.wait_ge(first_idx, 32)
            cast_dst(0)
            statistics(0, 0)
            combine(0, 0)
            dve.wait_ge(consts, 6)
            dve.wait_ge(rows_loaded, 32)
            planned(nc.vector.tensor_reduce(out=least[:, :], in_=dst_rows[:, :], axis=AX.X, op=ALU.min))
            planned(nc.vector.tensor_scalar(least_pair[:, :], least[:, :], (2 * G).bit_length() - 1, None, ALU.arith_shift_right))
            planned(nc.vector.tensor_tensor(need[:, 0:1], group_no[:, :], least_pair[:, :], ALU.subtract))
            nc.vector.tensor_reduce(out=need[:, 1:2], in_=dst_rows[:, :], axis=AX.X, op=ALU.max).then_inc(need_set, 1)
            dve.wait_ge(need_turned, 1)
            planned(nc.vector.tensor_reduce(out=plan[:, 0:1], in_=sumps[0:1, 0:EG + 1], axis=AX.X, op=ALU.max))
            planned(nc.vector.tensor_scalar(plan[:, 1:2], plan[:, 0:1], float(LAG), float(FIRST), ALU.add, ALU.max))
            planned(nc.vector.tensor_scalar(plan[:, 2:3], plan[:, 1:2], float(MOST), float(EG + 1), ALU.is_gt, ALU.mult))
            planned(nc.vector.tensor_tensor(plan[:, 3:4], plan[:, 1:2], plan[:, 2:3], ALU.max))
            planned(nc.vector.tensor_scalar(plan[:, 3:4], plan[:, 3:4], float(EG + 1), None, ALU.min))
            planned(nc.vector.tensor_scalar(plan[:, 4:5], plan[:, 3:4], float(EG - 1), None, ALU.min))
            planned(nc.vector.tensor_scalar(ctrl[:, 0:1], plan[:, 3:4], float(-FIRST), None, ALU.add))
            planned(nc.vector.tensor_scalar(ctrl[:, 1:2], plan[:, 4:5], float(-FIRST), None, ALU.add))
            planned(nc.vector.tensor_scalar(plan[:, 5:6], plan[:, 3:4], -1.0, float(EG), ALU.mult, ALU.add))
            planned(nc.vector.tensor_scalar(ctrl[:, 2:3], plan[:, 5:6], 0.0, None, ALU.max))
            planned(nc.vector.tensor_scalar(ctrl[:, 3:4], plan[:, 5:6], -1.0, 0.0, ALU.add, ALU.max))
            planned(nc.vector.tensor_scalar(plan[:, 4:8], sumps[0:1, P:P + FIRST], float(LOW), 16.0, ALU.is_ge, ALU.mult))
            nc.vector.tensor_scalar(ctrl[:, 4:4 + FIRST], plan[:, 4:8], 1.0, None, ALU.add).then_inc(ctrl_set, 1)
            planned(nc.vector.tensor_scalar(rank_f[:, :], rank_bits[:, :], 1, 23, ALU.arith_shift_right, ALU.logical_shift_left))
            nc.vector.tensor_copy(rank[:, :], rank_f[:, :].bitcast(F32))
            nc.vector.tensor_scalar(rank2[:, :], rank_f[:, 0:1].bitcast(F32), 2.0, None, ALU.mult).then_inc(ranked, 1)
            dve.wait_ge(idx_loaded, 64)
            dve.wait_ge(loaded, LOADS)
            for n in range(2):
                planned(nc.vector.tensor_copy(w1hi[n][:, :, :], w1[n][:, :, :]))
                last = nc.vector.tensor_tensor(w1lo[n][:, :, :], w1[n][:, :, :], w1hi[n][:, :, :].bitcast(F32), ALU.subtract)
            last.then_inc(split, 1)

            def is_int(e, n):
                return isinstance(e, int) and e == n

            def edge_step(e):
                if not is_int(e, 0):
                    cast_dst(e, is_int(e, EG))
                    statistics(0, e)
                    combine(0, e)
                invert(0, e)
                normalise_edges(e)
                low_edges(e)
                mark_same(e)
                rows_to_add(e)
                edge_results(e, e)
                low_rel(e, e)

            def node_statistics(j):
                for r in (1, 2):
                    statistics(r, j)
                for r in (1, 2):
                    combine(r, j)

            def node_inverses(j):
                for r in (1, 2):
                    invert(r, j)
                for r in (1, 2):
                    shifts(r, j)

            def enter(lead):
                cast_dst(lead)
                statistics(0, lead)
                combine(0, lead)
                invert(0, lead)
                normalise_edges(lead)
                node_statistics(0)
                low_edges(lead)
                node_inverses(0)

            def enter_alone():
                node_statistics(0)
                node_inverses(0)

            def step(e, j, kind):
                turn = e + 2 * j
                more = kind < 2
                if more:
                    statistics(0, e + 1)
                    combine(0, e + 1)
                low_nodes(1, j)
                if more:
                    invert(0, e + 1)
                    normalise_edges(e + 1)
                mark_same(e)
                low_nodes(2, j)
                rows_to_add(e)
                if more:
                    cast_dst(e + 1, kind == 1)
                edge_results(e, turn)
                node_statistics(j + 1)
                low_rel(e, turn)
                if more:
                    low_edges(e + 1)
                node_inverses(j + 1)
                node_results(1, j, turn + 1)
                node_results(2, j, turn + 2)

            def pair_step(j, kind):
                turn = turn_alone(j)
                low_nodes(1, j)
                low_nodes(2, j)
                if kind != 2:
                    node_statistics(j + 1)
                    node_inverses(j + 1)
                node_results(1, j, turn)
                node_results(2, j, turn + 1)

            run(dve, edge_step, enter, step, pair_step, finish_edges=enter_alone)


_INS = ["x", "src", "dst", "edge_attr_128", "L0_gnn_re_w1", "L0_gnn_re_b1", "L0_gnn_re_w2", "L0_gnn_re_b2",
        "L0_gnn_ea_w1", "L0_gnn_ea_b1", "L0_gnn_ea_w2", "L0_gnn_ea_b2"]


def kernel(**inputs):
    import numpy as np
    import concourse.bacc as bacc
    from concourse.bass_utils import run_bass_kernel_spmd

    nc = bacc.Bacc("TRN2", target_bir_lowering=False, num_devices=1)
    arrays, args = {}, []
    for name in _INS:
        a = np.ascontiguousarray(inputs[name])
        arrays[f"in_{name}"] = a
        args.append(nc.dram_tensor(f"in_{name}", a.shape, mybir.dt.from_np(a.dtype), kind="ExternalInput").ap())
    out = nc.dram_tensor("out", arrays["in_x"].shape, F32, kind="ExternalOutput").ap()
    gnn_program(nc, *args, out)
    r = run_bass_kernel_spmd(nc, [arrays], core_ids=[0])
    return r.results[0]["out"]
```

```python
import concourse.bass as bass
from concourse import mybir
from contextlib import ExitStack

P = 128
F32 = mybir.dt.float32
F32R = mybir.dt.float32r
I32 = mybir.dt.int32
ALU = mybir.AluOpType
ACT = mybir.ActivationFunctionType
AX = mybir.AxisListType


def gnn_program(nc, x, src, dst, ea, re_w1, re_b1, re_w2, re_b2, ea_w1, ea_b1, ea_w2, ea_b2, out):
    N, D = x.shape
    E = src.shape[0]
    HID = re_w1.shape[1]
    C = HID // P
    T = 4
    G = T * P
    EG = E // G
    EDGE_TAIL = E - G
    DONE = (EG * G - EDGE_TAIL) // T
    NP = N // (2 * G)
    NODE_TAIL = N - 2 * G
    SPARE = N
    EPS = 1e-5
    LOADS = 16 * (3 + C)
    LAG = 3
    FIRST = 4
    MOST = EG - 4
    STRIP = 2 * G
    STRIPS = EG - 1 - FIRST
    LOW = N - STRIPS * STRIP
    LOW_PARTS = 4
    PARTS = 24
    SHIFT = STRIP.bit_length() - 1
    assert (EG * G - EDGE_TAIL) % T == 0 and D == P and EG * G < E and NP * 2 * G < N and NP == EG
    assert FIRST > LAG and STRIP == 1 << SHIFT and LOW % LOW_PARTS == 0

    agg = nc.dram_tensor("agg", [N + P, D], F32, kind="Internal").ap()

    ctx = ExitStack()
    with ctx:
        def sb(name, shape, dt=F32):
            return ctx.enter_context(nc.sbuf_tensor(name, shape, dt))

        def ps(name, shape):
            return ctx.enter_context(nc.psum_tensor(name, shape, F32))

        def sem(name):
            return ctx.enter_context(nc.semaphore(name))

        w1 = [sb("w1e", [P, 3, HID]), sb("w1n", [P, 2, HID])]
        w1hi = [sb("w1e_hi", [P, 3, HID], F32R), sb("w1n_hi", [P, 2, HID], F32R)]
        w1lo = [sb("w1e_lo", [P, 3, HID], F32R), sb("w1n_lo", [P, 2, HID], F32R)]
        w2 = [sb("w2e", [P, C, D]), sb("w2n", [P, C, D])]
        b1 = [sb("b1e", [P, C]), sb("b1n", [P, C])]
        b2e = sb("b2e", [P, D])
        b2n = sb("b2n", [P, D])
        ident = sb("ident", [P, P])
        earlier = sb("earlier", [P, P])
        spare = sb("spare", [P, 1])
        eps = sb("eps", [P, 1])
        ZQ = 1024
        zeros = sb("zeros", [P, ZQ])
        dst_rows = sb("dst_rows", [EG + 1, G], I32)
        least = sb("least", [EG + 1, 1], I32)
        least_pair = sb("least_pair", [EG + 1, 1], I32)
        group_no = sb("group_no", [EG + 1, 1])
        most = sb("most", [EG + 1, 2], I32)
        most_strip = sb("most_strip", [EG + 1, 1], I32)
        ahead = sb("ahead", [EG + 1, 1])
        need = sb("need", [EG + 1, 3])
        plan = sb("plan", [1, 8])
        waits = sb("waits", [1, EG + 1])
        WAITS = 7
        ctrl = sb("ctrl", [1, WAITS + EG + 1], I32)
        src_all = sb("src_all", [P, EG + 1, T], I32)
        dst_all = sb("dst_all", [P, EG + 1, T], I32)
        gidx = [sb(f"gidx{b}", [P, 2, T], I32) for b in range(2)]
        sidx_new = [sb(f"sidx_new{b}", [P, T], I32) for b in range(FIRST)]
        sidx = sb("sidx", [P, T], I32)
        gath = [sb(f"gath{b}", [P, 2, T, D]) for b in range(2)]
        ea_in = [sb(f"ea_in{b}", [P, T, D]) for b in range(2)]
        dst_bc = sb("dst_bc", [P, 2, G], I32)
        dstf = sb("dstf", [P, EG + 1, T])
        off = sb("off", [P, EG + 1, T])
        same = sb("same", [P, T, P], F32R)
        masked = sb("masked", [P, T, P])
        repeats = sb("repeats", [P, T])
        off2 = sb("off2", [P, T])
        rel = sb("rel", [P, T, D])
        rel_parts = sb("rel_parts", [P, T, 2, D], F32R)
        losum = sb("losum", [P, T, D])
        relsum_new = sb("relsum_new", [P, T, D])
        relsum = [sb(f"relsum{b}", [P, T, D]) for b in range(FIRST)]
        tiles = [2 * T, T, T]
        parts = [3, 2, 2]
        order = [(2, 0, 1), (1, 0), (1, 0)]
        h = [sb(f"h{r}", [P, tiles[r], D]) for r in range(3)]
        st = [sb(f"st{r}", [P, tiles[r], 6]) for r in range(3)]
        mv = [sb(f"mv{r}", [P, tiles[r], 2]) for r in range(3)]
        sd = [sb(f"sd{r}", [P, tiles[r]]) for r in range(3)]
        rs = [sb(f"rs{r}", [P, tiles[r]]) for r in range(3)]
        shift = [None] + [sb(f"shift{r}", [P, T]) for r in (1, 2)]
        hi = [sb(f"hi{r}", [P, parts[r], G], F32R) for r in range(3)]
        lo = [sb(f"lo{r}", [P, parts[r], G], F32R) for r in range(3)]
        hid = [sb(f"hid{r}", [P, C, G]) for r in range(3)]
        xin = [None] + [sb(f"xin{r}", [P, T, D]) for r in (1, 2)]
        xb = [None] + [sb(f"xb{r}", [P, T, D]) for r in (1, 2)]
        agg_in = [None] + [sb(f"agg_in{r}", [P, T, D]) for r in (1, 2)]
        res = [None] + [sb(f"res{r}", [P, T, D]) for r in (1, 2)]

        tps = [ps(f"tps{b}", [P, G]) for b in range(3)]
        l1ps = [ps(f"l1ps{c}", [P, G]) for c in range(C)]
        l2ps = ps("l2ps", [P, G])
        sumps = [ps(f"sumps{b}", [P, G]) for b in range(2)]

        loaded = [sem("loaded_e"), sem("loaded_n")]
        first_idx = sem("first_idx")
        idx_loaded = sem("idx_loaded")
        rows_loaded = sem("rows_loaded")
        consts = sem("consts")
        low_zeroed = sem("low_zeroed")
        zeroed = sem("zeroed")
        all_zeroed = sem("all_zeroed")
        zeros_set = sem("zeros_set")
        whi_set = sem("whi_set")
        split = [sem("split_e"), sem("split_n")]
        planning = sem("planning")
        need_set = sem("need_set")
        need_turned = sem("need_turned")
        ctrl_set = sem("ctrl_set")
        gidx_set = sem("gidx_set")
        gathered = [[sem(f"gathered{b}_{k}") for k in range(T)] for b in range(2)]
        ea_loaded = [sem(f"ea_loaded{b}") for b in range(2)]
        bc_loaded = [sem(f"bc_loaded{b}") for b in range(2)]
        ea_used = sem("ea_used")
        scattered = sem("scattered")
        dstf_cast = sem("dstf_cast")
        dstf_set = sem("dstf_set")
        tail_cut = sem("tail_cut")
        same_set = sem("same_set")
        repeats_set = sem("repeats_set")
        off2_set = sem("off2_set")
        sidx_set = sem("sidx_set")
        sidx_kept = sem("sidx_kept")
        relhi_set = sem("relhi_set")
        rello_set = sem("rello_set")
        summed = sem("summed")
        losum_set = sem("losum_set")
        relnew_set = sem("relnew_set")
        relsum_set = sem("relsum_set")
        stats = [sem(f"stats{r}") for r in range(3)]
        moments = [sem(f"moments{r}") for r in range(3)]
        deviation = [sem(f"deviation{r}") for r in range(3)]
        inverse = [sem(f"inverse{r}") for r in range(3)]
        shift_set = [None] + [sem(f"shift_set{r}") for r in (1, 2)]
        normed = [sem(f"normed{r}") for r in range(3)]
        transposed = [sem(f"transposed{r}") for r in range(3)]
        hi_set = [sem(f"hi_set{r}") for r in range(3)]
        lo_set = [sem(f"lo_set{r}") for r in range(3)]
        x_loaded = [None] + [sem(f"x_loaded{r}") for r in (1, 2)]
        xb_set = [None] + [sem(f"xb_set{r}") for r in (1, 2)]
        agg_loaded = [None] + [sem(f"agg_loaded{r}") for r in (1, 2)]
        agg_used = [None] + [sem(f"agg_used{r}") for r in (1, 2)]
        stored = [None] + [sem(f"stored{r}") for r in (1, 2)]
        l1_done = sem("l1_done")
        hid_set = sem("hid_set")
        l2_done = sem("l2_done")
        results = sem("results")
        pool_passed = sem("pool_passed")
        dve_passed = sem("dve_passed")

        def rows(t, start):
            return t[bass.ds(start, G), :].rearrange("(p k) f -> p k f", k=T)

        def tiled(t):
            return t[:, :].rearrange("p (k f) -> p k f", k=T)

        def half(b, part):
            return sumps[b][:, :].rearrange("p (k h f) -> p k h f", k=2, h=2)[:, :, part, :]

        def wait(eng, s, value):
            if not isinstance(value, int) or value > 0:
                eng.wait_ge(s, value)

        def read_plan(eng):
            eng.wait_ge(ctrl_set, 1)
            lead = FIRST + eng.value_load(ctrl[0:1, 0:1], min_val=0, max_val=EG + 1 - FIRST)
            bound = FIRST + eng.value_load(ctrl[0:1, 1:2], min_val=0, max_val=EG - 1 - FIRST)
            alone = 1 + eng.value_load(ctrl[0:1, 2:3], min_val=0, max_val=EG - FIRST)
            joint = eng.value_load(ctrl[0:1, 3:4], min_val=0, max_val=EG - 1 - FIRST)
            return eng.snap(lead), eng.snap(bound), eng.snap(alone), joint

        def nothing(*_):
            pass

        def run(eng, edge_step, enter, step, enter_pairs, pair_step):
            for e in range(FIRST):
                edge_step(e)
            lead, bound, alone, joint = read_plan(eng)
            with eng.If(lead > FIRST):
                with eng.Fori(FIRST, bound) as e:
                    edge_step(e)
            with eng.If(lead < EG + 1):
                few = lead.with_bounds(min_val=FIRST, max_val=MOST)
                enter(few + (1 - LAG))
                step(few, 0, 0)
                with eng.Fori(1, joint) as j:
                    step((few + j).with_bounds(min_val=FIRST + 1, max_val=EG - 2), j, 0)
                step(EG - 1, joint, 1)
                step(EG, joint + 1, 2)
                enter_pairs(alone)
            with eng.Else():
                edge_step(EG - 1)
                edge_step(EG)
                enter(EG + 1)
                enter_pairs(0)
                pair_step(0, 4)
            pair_step(alone, 3)
            with eng.Fori(alone + 1, NP - 1) as j:
                pair_step(j, 0)
            pair_step(NP - 1, 1)
            pair_step(NP, 2)

        def early(e):
            return isinstance(e, int) and e < FIRST

        def slot(e):
            if isinstance(e, int) and e < FIRST:
                return e % 2, e // 2 + 1
            return 0, e - FIRST // 2 + 1

        def before(e):
            return e - 2 if isinstance(e, int) and e <= FIRST else e - 1

        def sum_buffer(e):
            return FIRST - 1 - e if early(e) else 0

        def turn_alone(j):
            return EG + 1 + 2 * j

        block = ctx.enter_context(nc.Block())

        @block.sync
        def _(sp):
            for side, t in ((src, src_all), (dst, dst_all)):
                whole = side[0:EG * G].rearrange("(g p k) -> p g k", p=P, k=T)
                sp.dma_start(t[:, 0:2, :], whole[:, 0:2, :]).then_inc(first_idx, 16)
            def load_weights(n, weight1, bias1, weight2, bias2):
                sp.dma_start(w1[n][:, :, :], weight1.rearrange("(c p) n -> p c n", p=P)).then_inc(loaded[n], 16)
                for c in range(C):
                    sp.dma_start(b1[n][:, c:c + 1], bias1[c * P:(c + 1) * P].unsqueeze(1)).then_inc(loaded[n], 16)
                sp.dma_start(w2[n][:, :, :], weight2.rearrange("(c p) n -> p c n", p=P)).then_inc(loaded[n], 16)
                sp.dma_start((b2e, b2n)[n][:, :], bias2.unsqueeze(0).to_broadcast([P, D])).then_inc(loaded[n], 16)

            def zero(start, count, to):
                n = count * D // P
                q = next(q for q in range(ZQ, 0, -1) if n % q == 0)
                flat = agg[bass.ds(start, count), :].rearrange("n f -> (n f)").rearrange("(p r q) -> p r q", r=n // q, q=q)
                sp.dma_start(flat, zeros[:, 0:q].unsqueeze(1).to_broadcast([P, n // q, q])).then_inc(to, 16)

            def load_ea(e, start):
                b, n = slot(e)
                prior = before(e)
                wait(sp, ea_used, prior + 1)
                wait(sp, same_set, prior + 1)
                sp.dma_start(ea_in[b][:, :, :], rows(ea, start)).then_inc(ea_loaded[b], 16)
                sp.dma_start(dst_bc[:, b, :], dst[bass.ds(start, G)].unsqueeze(0).to_broadcast([P, G])).then_inc(bc_loaded[b], 16)

            def load_x(j, start):
                for r in (1, 2):
                    wait(sp, normed[r], j * T)
                    wait(sp, xb_set[r], j)
                    sp.dma_start(xin[r][:, :, :], rows(x, start + (r - 1) * G)).then_inc(x_loaded[r], 16)

            def load_agg(j, start, edges):
                for r in (1, 2):
                    wait(sp, scattered, 16 * T * edges)
                    wait(sp, agg_used[r], j)
                    sp.dma_start(agg_in[r][:, :, :], rows(agg, start + (r - 1) * G)).then_inc(agg_loaded[r], 16)

            def store(r, start, turn):
                sp.wait_ge(results, turn + r)
                sp.dma_start(rows(out, start + (r - 1) * G), res[r][:, :, :]).then_inc(stored[r], 16)

            load_ea(0, 0)
            load_weights(0, re_w1, re_b1, re_w2, re_b2)
            sp.dma_start(dst_rows[0:EG, :], dst[0:EG * G].rearrange("(g n) -> g n", n=G)).then_inc(rows_loaded, 16)
            sp.dma_start(dst_rows[EG:EG + 1, :], dst[EDGE_TAIL:E].unsqueeze(0)).then_inc(rows_loaded, 16)
            sp.wait_ge(gathered[0][T - 2], 32)
            for side, t in ((src, src_all), (dst, dst_all)):
                whole = side[0:EG * G].rearrange("(g p k) -> p g k", p=P, k=T)
                sp.dma_start(t[:, 2:EG, :], whole[:, 2:EG, :]).then_inc(idx_loaded, 16)
                sp.dma_start(t[:, EG, :], side[EDGE_TAIL:E].rearrange("(p k) -> p k", k=T)).then_inc(idx_loaded, 16)
            load_ea(1, G)
            sp.wait_ge(gathered[1][T - 1], 32)
            load_weights(1, ea_w1, ea_b1, ea_w2, ea_b2)
            load_x(0, 0)
            sp.wait_ge(zeros_set, 1)
            for z in range(LOW_PARTS):
                zero(z * LOW // LOW_PARTS, LOW // LOW_PARTS, low_zeroed)
            zero(SPARE, P, low_zeroed)
            load_ea(2, 2 * G)
            sp.wait_ge(ctrl_set, 1)
            in_strips = sp.value_load(ctrl[0:1, 4:5], min_val=0, max_val=1)
            zeroed_end = sp.value_load(ctrl[0:1, 5:6], min_val=1, max_val=16 * STRIPS + 1)
            all_zeroed_end = sp.value_load(ctrl[0:1, 6:7], min_val=1, max_val=16 * PARTS + 1)
            with sp.If(in_strips < 1):
                for z in range(PARTS):
                    start = LOW + z * (N - LOW) // PARTS
                    zero(start, LOW + (z + 1) * (N - LOW) // PARTS - start, all_zeroed)

            def zero_strip(e):
                with sp.If(in_strips > 0):
                    sp.wait_ge(zeroed, 16 * (e - FIRST) + 1)
                    zero(LOW + (e - FIRST) * STRIP, STRIP, zeroed)

            def edge_step(e):
                if not isinstance(e, int):
                    zero_strip(e)
                    load_ea(e + 1, (e + 1) * G)
                elif 1 <= e < FIRST - 1:
                    load_ea(e + 2, (e + 2) * G)
                elif e == EG - 1:
                    load_ea(EG, EDGE_TAIL)

            def enter(edges):
                sp.wait_ge(all_zeroed, all_zeroed_end)
                load_agg(0, 0, edges)

            def step(e, j, kind):
                if kind == 0:
                    zero_strip(e)
                load_x(j + 1, (j + 1) * 2 * G)
                if kind < 2:
                    load_ea(e + 1, EDGE_TAIL if kind else (e + 1) * G)
                load_agg(j + 1, (j + 1) * 2 * G, e + 2 - LAG)
                for r in (1, 2):
                    store(r, j * 2 * G, e + 2 * j + 1)

            def pair_step(j, kind):
                if kind != 2:
                    start = NODE_TAIL if kind == 1 else (j + 1) * 2 * G
                    load_x(j + 1, start)
                if kind < 3:
                    store(2, (j - 1) * 2 * G, turn_alone(j - 1))
                if kind == 2:
                    for r in (1, 2):
                        sp.wait_ge(stored[r], 16 * NP)
                    for r in (1, 2):
                        store(r, NODE_TAIL, turn_alone(j))
                else:
                    load_agg(j + 1, start, EG if kind == 3 else EG + 1)
                    store(1, j * 2 * G, turn_alone(j))
                    if kind == 4:
                        store(2, j * 2 * G, turn_alone(j))

            run(sp, edge_step, enter, step, nothing, pair_step)
            for r in (1, 2):
                sp.wait_ge(stored[r], 16 * (NP + 1))
            sp.wait_ge(low_zeroed, 16 * (LOW_PARTS + 1))
            sp.wait_ge(zeroed, zeroed_end)
            sp.wait_ge(all_zeroed, all_zeroed_end)

        @block.gpsimd
        def _(pool):
            pool.sem_inc(zeroed, 1)
            pool.sem_inc(all_zeroed, 1)
            nc.gpsimd.memset(ident[:, :], 0.0).then_inc(consts, 1)
            nc.gpsimd.memset(eps[:, :], EPS).then_inc(consts, 1)
            nc.gpsimd.memset(earlier[:, :], 1.0).then_inc(consts, 1)
            nc.gpsimd.iota(spare[:, :], pattern=[[0, 1]], base=SPARE, channel_multiplier=1,
                           allow_small_or_imprecise_dtypes=True).then_inc(consts, 1)
            nc.gpsimd.iota(group_no[:, :], pattern=[[0, 1]], base=0, channel_multiplier=1,
                           allow_small_or_imprecise_dtypes=True).then_inc(consts, 1)
            pool.wait_ge(consts, 5)
            nc.gpsimd.affine_select(out=ident[:, :], in_=ident[:, :], compare_op=ALU.not_equal, fill=1.0,
                                    base=0, pattern=[[-1, P]], channel_multiplier=1).then_inc(consts, 1)
            nc.gpsimd.affine_select(out=earlier[:, :], in_=earlier[:, :], compare_op=ALU.is_gt, fill=0.0,
                                    base=0, pattern=[[-1, P]], channel_multiplier=1).then_inc(consts, 1)
            pool.wait_ge(first_idx, 32)

            def copy_gidx(e):
                b, n = slot(e)
                for k in range(T):
                    wait(pool, gathered[b][k], 32 * (n - 1))
                pool.sem_inc(pool_passed, 1)
                nc.gpsimd.tensor_copy(gidx[b][:, 0, :], src_all[:, e, :])
                nc.gpsimd.tensor_copy(gidx[b][:, 1, :], dst_all[:, e, :]).then_inc(gidx_set, 1)
                pool.wait_ge(gidx_set, e + 1)

            def gather(e, k):
                b, n = slot(e)
                prior = before(e)
                if not isinstance(e, int) or prior >= 0:
                    pool.wait_ge(normed[0], T * prior + k + 1)
                pool.sem_inc(pool_passed, 1)
                for s in range(2):
                    nc.gpsimd.indirect_dma_start(
                        gath[b][:, s, k, :], None, x,
                        bass.IndirectOffsetOnAxis(ap=gidx[b][:, s, k:k + 1], axis=0)).then_inc(gathered[b][k], 16)

            def scatter(e, k):
                if k == 0:
                    pool.wait_ge(relsum_set, e + 1)
                    pool.wait_ge(sidx_set, e + 1)
                    wait(pool, scattered, 16 * T * e)
                    pool.sem_inc(pool_passed, 1)
                    nc.gpsimd.tensor_copy(sidx[:, :], sidx_new[sum_buffer(e)][:, :]).then_inc(sidx_kept, 1)
                    pool.wait_ge(sidx_kept, e + 1)
                    if isinstance(e, int) and e == 0:
                        pool.wait_ge(ctrl_set, 1)
                        pool.wait_ge(low_zeroed, 16 * (LOW_PARTS + 1))
                        pool.wait_ge(all_zeroed, pool.value_load(ctrl[0:1, 6:7], min_val=1, max_val=16 * PARTS + 1))
                    pool.sem_inc(pool_passed, 1)
                    strips_needed = pool.value_load(ctrl[0:1, bass.ds(WAITS + e, 1)], min_val=1, max_val=16 * STRIPS + 1)
                    pool.wait_ge(zeroed, strips_needed)
                wait(pool, scattered, 16 * (T * e + k))
                pool.sem_inc(pool_passed, 1)
                nc.gpsimd.indirect_dma_start(
                    agg, bass.IndirectOffsetOnAxis(ap=sidx[:, k:k + 1], axis=0),
                    relsum[sum_buffer(e)][:, k, :], None, compute_op=ALU.add).then_inc(scattered, 16)

            def keep_x(r, j, before):
                pool.wait_ge(x_loaded[r], 16 * (j + 1))
                wait(pool, results, before)
                nc.gpsimd.tensor_tensor(xb[r][:, :, :], xin[r][:, :, :],
                                        b2n[:, :].unsqueeze(1).to_broadcast([P, T, D]), ALU.add).then_inc(xb_set[r], 1)

            copy_gidx(0)
            for k in range(T):
                gather(0, k)
            copy_gidx(1)
            for k in range(T):
                gather(1, k)
            pool.wait_ge(idx_loaded, 64)

            def edge_step(e, joint=False):
                more = not isinstance(e, int) or e + 2 <= EG
                mixed = joint or early(e)
                if more and mixed:
                    copy_gidx(e + 2)
                if isinstance(e, int) and e == 1:
                    pool.wait_ge(loaded[1], LOADS)
                    for r in (1, 2):
                        keep_x(r, 0, 0)
                for k in range(T):
                    if not isinstance(e, int) or e > 0:
                        scatter(e - 1, k)
                    if more and mixed:
                        gather(e + 2, k)
                if more and not mixed:
                    copy_gidx(e + 2)
                    for k in range(T):
                        gather(e + 2, k)

            def step(e, j, kind):
                if not isinstance(j, int) or j > 0:
                    keep_x(1, j, e + 2 * j - 1)
                    keep_x(2, j, e + 2 * j)
                edge_step(e, joint=True)

            def keep_pair(j):
                keep_x(1, j, turn_alone(j) - 1)
                keep_x(2, j, turn_alone(j))

            def enter_pairs(j):
                if not isinstance(j, int) or j > 0:
                    keep_pair(j)
                for k in range(T):
                    scatter(EG, k)

            def pair_step(j, kind):
                if kind != 2:
                    keep_pair(j + 1)

            run(pool, edge_step, nothing, step, enter_pairs, pair_step)

        @block.tensor
        def _(pe):
            def transpose_edges(e):
                b, n = slot(e)
                pe.wait_ge(ea_loaded[b], 16 * n)
                for k in range(T):
                    last = nc.tensor.transpose(tps[2][:, k * P:(k + 1) * P], ea_in[b][:, k, :], ident[:, :])
                last.then_inc(ea_used, 1)
                for k in range(T):
                    pe.wait_ge(normed[0], T * e + k + 1)
                    for s in range(2):
                        last = nc.tensor.transpose(tps[s][:, k * P:(k + 1) * P], h[0][:, s * T + k, :], ident[:, :])
                last.then_inc(transposed[0], 1)

            def transpose_nodes(r, j):
                pe.wait_ge(agg_loaded[r], 16 * (j + 1))
                for k in range(T):
                    last = nc.tensor.transpose(tps[1][:, k * P:(k + 1) * P], agg_in[r][:, k, :], ident[:, :])
                last.then_inc(agg_used[r], 1)
                pe.wait_ge(normed[r], T * (j + 1))
                for k in range(T):
                    last = nc.tensor.transpose(tps[0][:, k * P:(k + 1) * P], h[r][:, k, :], ident[:, :])
                last.then_inc(transposed[r], 1)

            def layer1(r, n, turn, c):
                K = parts[r]
                w = min(r, 1)
                wait(pe, hid_set, C * (turn - 1) + c + 1 if not isinstance(turn, int) or turn > 0 else 0)
                for i, q in enumerate(order[r]):
                    if c == 0:
                        pe.wait_ge(hi_set[r], K * n + i + 1)
                    for part in (w1hi[w], w1lo[w]):
                        nc.tensor.matmul(l1ps[c][:, :], part[:, q, c * P:(c + 1) * P], hi[r][:, q, :],
                                         start=(i == 0 and part is w1hi[w]), stop=False)
                if c == 0:
                    pe.wait_ge(lo_set[r], n + 1)
                for q in range(K):
                    last = nc.tensor.matmul(l1ps[c][:, :], w1hi[w][:, q, c * P:(c + 1) * P], lo[r][:, q, :],
                                            start=False, stop=(q == K - 1))
                last.then_inc(l1_done, 1)

            def layer2(r, turn):
                pe.wait_ge(hid_set, C * (turn + 1))
                wait(pe, results, turn)
                w = w2[min(r, 1)]
                for k in range(T):
                    for c in range(C):
                        last = nc.tensor.matmul(l2ps[:, k * P:(k + 1) * P], hid[r][:, c, k * P:(k + 1) * P],
                                                w[:, c, :], start=(c == 0), stop=(c == C - 1))
                last.then_inc(l2_done, 1)

            def sum_same(e):
                pe.wait_ge(rello_set, e + 1)
                pe.wait_ge(same_set, e + 1)
                wait(pe, relnew_set, e)
                for k in range(T):
                    last = nc.tensor.matmul(sumps[k // 2][:, k % 2 * 2 * D:(k % 2 + 1) * 2 * D], same[:, k, :],
                                            rel_parts[:, k, :, :], start=True, stop=True)
                last.then_inc(summed, 1)

            def edge_step(e):
                layer1(0, e, e, 0)
                layer1(0, e, e, 1)
                layer2(0, e)
                if not isinstance(e, int) or e < EG:
                    transpose_edges(e + 1)
                sum_same(e)

            def step(e, j, kind):
                turn = e + 2 * j
                layer1(0, e, turn, 0)
                transpose_nodes(1, j)
                layer1(0, e, turn, 1)
                layer1(1, j, turn + 1, 0)
                transpose_nodes(2, j)
                layer1(1, j, turn + 1, 1)
                layer2(0, turn)
                layer1(2, j, turn + 2, 0)
                layer2(1, turn + 1)
                layer1(2, j, turn + 2, 1)
                sum_same(e)
                if kind < 2:
                    transpose_edges(e + 1)
                layer2(2, turn + 2)

            def enter_pairs(j):
                transpose_nodes(1, j)

            def pair_step(j, kind):
                turn = turn_alone(j)
                layer1(1, j, turn, 0)
                transpose_nodes(2, j)
                layer1(1, j, turn, 1)
                layer1(2, j, turn + 1, 0)
                layer1(2, j, turn + 1, 1)
                layer2(1, turn)
                if kind != 2:
                    transpose_nodes(1, j + 1)
                layer2(2, turn + 1)

            pe.wait_ge(consts, 7)
            pe.wait_ge(need_set, 1)
            for n in range(3):
                last = nc.tensor.transpose(sumps[0][0:1, n * P:n * P + EG + 1], need[:, n:n + 1], ident[0:EG + 1, 0:EG + 1])
            last.then_inc(need_turned, 1)
            transpose_edges(0)
            pe.wait_ge(loaded[0], LOADS)
            pe.wait_ge(split[0], 1)

            def enter(edges):
                pe.wait_ge(split[1], 1)

            run(pe, edge_step, enter, step, enter_pairs, pair_step)

        @block.scalar
        def _(act):
            def deviations(r, n):
                act.wait_ge(moments[r], n + 1)
                nc.scalar.activation(sd[r][:, :], mv[r][:, :, 1], ACT.Sqrt, bias=eps[:, 0:1]).then_inc(deviation[r], 1)

            def high_edges(e):
                act.wait_ge(ea_used, e + 1)
                nc.scalar.activation(hi[0][:, 2, :], tps[2][:, :], ACT.Copy).then_inc(hi_set[0], 1)
                act.wait_ge(transposed[0], e + 1)
                for q in range(2):
                    nc.scalar.activation(hi[0][:, q, :], tps[q][:, :], ACT.Relu).then_inc(hi_set[0], 1)

            def high_nodes(r, j):
                act.wait_ge(agg_used[r], j + 1)
                nc.scalar.activation(hi[r][:, 1, :], tps[1][:, :], ACT.Copy).then_inc(hi_set[r], 1)
                act.wait_ge(transposed[r], j + 1)
                nc.scalar.activation(hi[r][:, 0, :], tps[0][:, :], ACT.Relu).then_inc(hi_set[r], 1)

            def hidden(r, turn, c, before):
                act.wait_ge(l1_done, C * turn + c + 1)
                if c == 0:
                    wait(act, l2_done, before)
                b = b1[min(r, 1)]
                nc.scalar.activation(hid[r][:, c, :], l1ps[c][:, :], ACT.Relu, bias=b[:, c:c + 1]).then_inc(hid_set, 1)

            def normalise(r, j):
                act.wait_ge(shift_set[r], j + 1)
                for k in range(T):
                    last = nc.scalar.activation(h[r][:, k, :], xin[r][:, k, :], ACT.Identity,
                                                bias=shift[r][:, k:k + 1], scale=rs[r][:, k:k + 1])
                last.then_inc(normed[r], T)

            def high_rel(e, turn):
                act.wait_ge(results, turn + 1)
                wait(act, summed, e)
                nc.scalar.activation(rel_parts[:, :, 0, :], rel[:, :, :], ACT.Copy).then_inc(relhi_set, 1)

            def low_sums(e):
                act.wait_ge(summed, e + 1)
                wait(act, relnew_set, e)
                for b in range(2):
                    last = nc.scalar.activation(losum[:, 2 * b:2 * b + 2, :], half(b, 1), ACT.Copy)
                last.then_inc(losum_set, 1)

            def sums(e):
                act.wait_ge(relnew_set, e + 1)
                wait(act, scattered, 16 * T * (0 if early(e) else e))
                nc.scalar.activation(relsum[sum_buffer(e)][:, :, :], relsum_new[:, :, :], ACT.Copy).then_inc(relsum_set, 1)

            act.wait_ge(consts, 7)
            deviations(0, 0)
            high_edges(0)
            act.wait_ge(loaded[0], LOADS)

            def edge_step(e):
                more = not isinstance(e, int) or e < EG
                hidden(0, e, 0, e)
                hidden(0, e, 1, e)
                if more:
                    deviations(0, e + 1)
                high_rel(e, e)
                if more:
                    high_edges(e + 1)
                low_sums(e)
                sums(e)
                if isinstance(e, int) and e == FIRST - 1:
                    for r in (1, 2):
                        deviations(r, 0)
                    normalise(1, 0)

            def enter(edges):
                act.wait_ge(loaded[1], LOADS)

            def step(e, j, kind):
                turn = e + 2 * j
                hidden(0, turn, 0, turn)
                high_nodes(1, j)
                normalise(2, j)
                first = isinstance(j, int) and j == 0
                if kind < 2 and not first:
                    deviations(0, e + 1)
                hidden(0, turn, 1, turn)
                hidden(1, turn + 1, 0, turn)
                high_nodes(2, j)
                if first:
                    deviations(0, e + 1)
                hidden(1, turn + 1, 1, turn)
                high_rel(e, turn)
                hidden(2, turn + 2, 0, turn)
                hidden(2, turn + 2, 1, turn)
                low_sums(e)
                deviations(1, j + 1)
                deviations(2, j + 1)
                if kind < 2:
                    high_edges(e + 1)
                normalise(1, j + 1)
                sums(e)

            def enter_pairs(j):
                high_nodes(1, j)
                normalise(2, j)

            def pair_step(j, kind):
                turn = turn_alone(j)
                hidden(1, turn, 0, turn - 1)
                high_nodes(2, j)
                hidden(1, turn, 1, turn - 1)
                hidden(2, turn + 1, 0, turn)
                if kind != 2:
                    deviations(1, j + 1)
                    deviations(2, j + 1)
                hidden(2, turn + 1, 1, turn)
                if kind != 2:
                    normalise(1, j + 1)
                    high_nodes(1, j + 1)
                    normalise(2, j + 1)

            run(act, edge_step, enter, step, enter_pairs, pair_step)

        @block.vector
        def _(dve):
            def statistics(r, n):
                for t in range(tiles[r]):
                    if r == 0 and t % 2 == 0:
                        b, count = slot(n)
                        dve.wait_ge(gathered[b][t // 2], 32 * count)
                    if r and t == 0:
                        dve.wait_ge(x_loaded[r], 16 * (n + 1))
                    last = nc.vector.bn_stats(st[r][:, t, :], source(r, n, t))
                last.then_inc(stats[r], 1)

            def combine(r, n):
                dve.wait_ge(stats[r], n + 1)
                dve.sem_inc(dve_passed, 1)
                for t in range(tiles[r]):
                    last = nc.vector.bn_aggr(mv[r][:, t, :], st[r][:, t, :])
                last.then_inc(moments[r], 1)

            def source(r, n, t):
                return xin[r][:, t, :] if r else gath[slot(n)[0]][:, t % 2, t // 2, :]

            def invert(r, n):
                dve.wait_ge(deviation[r], n + 1)
                nc.vector.reciprocal(rs[r][:, :], sd[r][:, :]).then_inc(inverse[r], 1)

            def normalise_edges(e):
                dve.wait_ge(inverse[0], e + 1)
                for t in range(2 * T):
                    last = nc.vector.tensor_scalar(h[0][:, (t % 2) * T + t // 2, :], source(0, e, t), mv[0][:, t, 0:1],
                                                   rs[0][:, t:t + 1], ALU.subtract, ALU.mult)
                    if t % 2:
                        last.then_inc(normed[0], 1)

            def shifts(r, j):
                dve.wait_ge(inverse[r], j + 1)
                nc.vector.scalar_tensor_tensor(out=shift[r][:, :], in0=mv[r][:, :, 0], scalar=-1.0, in1=rs[r][:, :],
                                               op0=ALU.mult, op1=ALU.mult).then_inc(shift_set[r], 1)

            def mark_same(e, tail=False):
                b, n = slot(e)
                dve.wait_ge(bc_loaded[b], 16 * n)
                if tail:
                    nc.vector.memset(dst_bc[:, b, 0:DONE * T], -1).then_inc(tail_cut, 1)
                    dve.wait_ge(tail_cut, 1)
                wait(dve, summed, e)
                nc.vector.tensor_tensor(same[:, :, :], dst_bc[:, b, :].rearrange("p (q k) -> p k q", k=T),
                                        dstf[:, e, :].unsqueeze(2).to_broadcast([P, T, P]), ALU.is_equal).then_inc(same_set, 1)

            def rows_to_add(e):
                dve.wait_ge(same_set, e + 1)
                for k in range(T):
                    last = nc.vector.tensor_tensor_reduce(masked[:, k, :], same[:, k, :], earlier[:, :], 1.0, 0.0,
                                                          ALU.mult, ALU.add, repeats[:, k:k + 1])
                last.then_inc(repeats_set, 1)
                dve.wait_ge(repeats_set, e + 1)
                nc.vector.scalar_tensor_tensor(out=off2[:, :], in0=repeats[:, :], scalar=0.5, in1=off[:, e, :],
                                               op0=ALU.is_ge, op1=ALU.mult).then_inc(off2_set, 1)
                dve.wait_ge(off2_set, e + 1)
                wait(dve, sidx_kept, 0 if early(e) else e)
                nc.vector.tensor_tensor(sidx_new[sum_buffer(e)][:, :], off2[:, :], dstf[:, e, :], ALU.add).then_inc(sidx_set, 1)

            def low_edges(e):
                for n, q in enumerate(order[0]):
                    dve.wait_ge(hi_set[0], 3 * e + n + 1)
                    if q == 2:
                        nc.vector.tensor_tensor(lo[0][:, q, :], tps[q][:, :], hi[0][:, q, :].bitcast(F32), ALU.subtract)
                    else:
                        last = nc.vector.scalar_tensor_tensor(out=lo[0][:, q, :], in0=tps[q][:, :], scalar=0.0,
                                                              in1=hi[0][:, q, :].bitcast(F32), op0=ALU.max, op1=ALU.subtract)
                last.then_inc(lo_set[0], 1)

            def low_nodes(r, j):
                dve.wait_ge(hi_set[r], 2 * j + 1)
                nc.vector.tensor_tensor(lo[r][:, 1, :], tps[1][:, :], hi[r][:, 1, :].bitcast(F32), ALU.subtract)
                dve.wait_ge(hi_set[r], 2 * j + 2)
                nc.vector.scalar_tensor_tensor(out=lo[r][:, 0, :], in0=tps[0][:, :], scalar=0.0,
                                               in1=hi[r][:, 0, :].bitcast(F32), op0=ALU.max, op1=ALU.subtract).then_inc(lo_set[r], 1)

            def edge_results(e, turn):
                dve.wait_ge(l2_done, turn + 1)
                wait(dve, relhi_set, e)
                wait(dve, rello_set, e)
                nc.vector.tensor_tensor(rel[:, :, :], tiled(l2ps),
                                        b2e[:, :].unsqueeze(1).to_broadcast([P, T, D]), ALU.add).then_inc(results, 1)

            def low_rel(e):
                dve.wait_ge(relhi_set, e + 1)
                wait(dve, summed, e)
                nc.vector.tensor_tensor(rel_parts[:, :, 1, :], rel[:, :, :], rel_parts[:, :, 0, :].bitcast(F32),
                                        ALU.subtract).then_inc(rello_set, 1)

            def add_parts(e):
                dve.wait_ge(losum_set, e + 1)
                wait(dve, relsum_set, e)
                for b in range(2):
                    last = nc.vector.tensor_tensor(relsum_new[:, 2 * b:2 * b + 2, :], half(b, 0),
                                                   losum[:, 2 * b:2 * b + 2, :], ALU.add)
                last.then_inc(relnew_set, 1)

            def node_results(r, j, turn):
                dve.wait_ge(l2_done, turn + 1)
                dve.wait_ge(xb_set[r], j + 1)
                wait(dve, stored[r], 16 * j)
                nc.vector.tensor_tensor(res[r][:, :, :], tiled(l2ps), xb[r][:, :, :], ALU.add).then_inc(results, 1)

            stages = [0]

            def end_stage(ins):
                stages[0] += 1
                ins.then_inc(planning, 1)
                dve.wait_ge(planning, stages[0])

            nc.vector.memset(zeros[:, :], 0.0).then_inc(zeros_set, 1)
            dve.wait_ge(consts, 7)
            dve.wait_ge(rows_loaded, 32)
            nc.vector.tensor_scalar(ahead[:, :], group_no[:, :], float(1 - FIRST), 0.0, ALU.add, ALU.max)
            nc.vector.tensor_reduce(out=least[:, :], in_=dst_rows[:, :], axis=AX.X, op=ALU.min)
            end_stage(nc.vector.tensor_reduce(out=most[:, 0:1], in_=dst_rows[:, :], axis=AX.X, op=ALU.max))
            nc.vector.tensor_scalar(least_pair[:, :], least[:, :], SHIFT, None, ALU.arith_shift_right)
            end_stage(nc.vector.tensor_scalar(most[:, 1:2], most[:, 0:1], float(STRIP - LOW), 0.0, ALU.add, ALU.max))
            nc.vector.tensor_tensor(need[:, 0:1], group_no[:, :], least_pair[:, :], ALU.subtract)
            end_stage(nc.vector.tensor_scalar(most_strip[:, :], most[:, 1:2], SHIFT, None, ALU.arith_shift_right))
            nc.vector.tensor_copy(need[:, 1:2], most_strip[:, :])
            nc.vector.tensor_tensor(need[:, 2:3], most_strip[:, :], ahead[:, :], ALU.subtract).then_inc(need_set, 1)

            def split_weights(n):
                dve.wait_ge(loaded[n], LOADS)
                nc.vector.tensor_copy(w1hi[n][:, :, :], w1[n][:, :, :]).then_inc(whi_set, 1)
                dve.wait_ge(whi_set, n + 1)
                nc.vector.tensor_tensor(w1lo[n][:, :, :], w1[n][:, :, :], w1hi[n][:, :, :].bitcast(F32),
                                        ALU.subtract).then_inc(split[n], 1)

            split_weights(0)
            statistics(0, 0)
            combine(0, 0)
            invert(0, 0)
            normalise_edges(0)

            dve.wait_ge(need_turned, 1)
            nc.vector.tensor_reduce(out=plan[:, 0:1], in_=sumps[0][0:1, 0:EG + 1], axis=AX.X, op=ALU.max)
            end_stage(nc.vector.tensor_reduce(out=plan[:, 1:2], in_=sumps[0][0:1, 2 * P:2 * P + EG + 1], axis=AX.X, op=ALU.max))
            nc.vector.tensor_scalar(plan[:, 2:3], plan[:, 0:1], float(LAG), float(FIRST), ALU.add, ALU.max)
            end_stage(nc.vector.tensor_scalar(plan[:, 3:4], plan[:, 1:2], 0.0, None, ALU.is_le))
            nc.vector.tensor_scalar(plan[:, 4:5], plan[:, 2:3], float(MOST), float(EG + 1), ALU.is_gt, ALU.mult)
            nc.vector.tensor_copy(ctrl[:, 4:5], plan[:, 3:4])
            nc.vector.tensor_scalar(ctrl[:, 5:6], plan[:, 3:4], 16.0 * STRIPS, 1.0, ALU.mult, ALU.add)
            nc.vector.tensor_scalar(ctrl[:, 6:7], plan[:, 3:4], -16.0 * PARTS, 16.0 * PARTS + 1, ALU.mult, ALU.add)
            end_stage(nc.vector.tensor_scalar(waits[:, :], sumps[0][0:1, P:P + EG + 1], plan[:, 3:4], 16.0, ALU.mult, ALU.mult))
            nc.vector.tensor_scalar(ctrl[:, WAITS:WAITS + EG + 1], waits[:, :], 1.0, None, ALU.add)
            end_stage(nc.vector.tensor_scalar(plan[:, 5:6], plan[:, 2:3], plan[:, 4:5], float(EG + 1), ALU.max, ALU.min))
            nc.vector.tensor_scalar(ctrl[:, 0:1], plan[:, 5:6], float(-FIRST), None, ALU.add)
            nc.vector.tensor_scalar(ctrl[:, 1:2], plan[:, 5:6], float(EG - 1), float(-FIRST), ALU.min, ALU.add)
            end_stage(nc.vector.tensor_scalar(plan[:, 6:7], plan[:, 5:6], -1.0, float(EG), ALU.mult, ALU.add))
            nc.vector.tensor_scalar(ctrl[:, 2:3], plan[:, 6:7], 0.0, None, ALU.max)
            nc.vector.tensor_scalar(ctrl[:, 3:4], plan[:, 6:7], -1.0, 0.0, ALU.add, ALU.max).then_inc(ctrl_set, 1)

            low_edges(0)
            dve.wait_ge(idx_loaded, 64)
            nc.vector.tensor_copy(dstf[:, :, :], dst_all[:, :, :]).then_inc(dstf_cast, 1)
            dve.wait_ge(dstf_cast, 1)
            nc.vector.tensor_copy(dstf[0:DONE, EG, :], spare[0:DONE, 0:1].to_broadcast([DONE, T])).then_inc(dstf_cast, 1)
            dve.wait_ge(dstf_cast, 2)
            nc.vector.tensor_scalar(off[:, :, :], dstf[:, :, :], -1.0, spare[:, 0:1], ALU.mult, ALU.add).then_inc(dstf_set, 1)
            dve.wait_ge(dstf_set, 1)

            def is_int(e, n):
                return isinstance(e, int) and e == n

            def node_statistics(j):
                for r in (1, 2):
                    statistics(r, j)
                for r in (1, 2):
                    combine(r, j)

            def node_inverses(j):
                for r in (1, 2):
                    invert(r, j)
                for r in (1, 2):
                    shifts(r, j)

            def edge_step(e):
                more = not is_int(e, EG)
                mark_same(e, is_int(e, EG))
                rows_to_add(e)
                if more:
                    statistics(0, e + 1)
                    combine(0, e + 1)
                edge_results(e, e)
                if more:
                    invert(0, e + 1)
                    normalise_edges(e + 1)
                low_rel(e)
                if more:
                    low_edges(e + 1)
                add_parts(e)
                if is_int(e, FIRST - 2):
                    split_weights(1)
                if is_int(e, FIRST - 1):
                    node_statistics(0)
                    node_inverses(0)

            def step(e, j, kind):
                turn = e + 2 * j
                more = kind < 2
                first = isinstance(j, int) and j == 0
                if first:
                    low_nodes(1, j)
                if more:
                    statistics(0, e + 1)
                    combine(0, e + 1)
                if first:
                    mark_same(e, kind == 2)
                    low_nodes(2, j)
                else:
                    low_nodes(1, j)
                if more:
                    invert(0, e + 1)
                    normalise_edges(e + 1)
                if not first:
                    mark_same(e, kind == 2)
                    low_nodes(2, j)
                if not first:
                    statistics(1, j + 1)
                edge_results(e, turn)
                rows_to_add(e)
                low_rel(e)
                if first:
                    statistics(1, j + 1)
                statistics(2, j + 1)
                node_results(1, j, turn + 1)
                for r in (1, 2):
                    combine(r, j + 1)
                add_parts(e)
                node_inverses(j + 1)
                if more:
                    low_edges(e + 1)
                node_results(2, j, turn + 2)

            def enter_pairs(j):
                low_nodes(1, j)

            def pair_step(j, kind):
                turn = turn_alone(j)
                low_nodes(2, j)
                if kind != 2:
                    node_statistics(j + 1)
                    node_inverses(j + 1)
                node_results(1, j, turn)
                if kind != 2:
                    low_nodes(1, j + 1)
                node_results(2, j, turn + 1)

            run(dve, edge_step, nothing, step, enter_pairs, pair_step)


_INS = ["x", "src", "dst", "edge_attr_128", "L0_gnn_re_w1", "L0_gnn_re_b1", "L0_gnn_re_w2", "L0_gnn_re_b2",
        "L0_gnn_ea_w1", "L0_gnn_ea_b1", "L0_gnn_ea_w2", "L0_gnn_ea_b2"]


def kernel(**inputs):
    import numpy as np
    import concourse.bacc as bacc
    from concourse.bass_utils import run_bass_kernel_spmd

    nc = bacc.Bacc("TRN2", target_bir_lowering=False, num_devices=1)
    arrays, args = {}, []
    for name in _INS:
        a = np.ascontiguousarray(inputs[name])
        arrays[f"in_{name}"] = a
        args.append(nc.dram_tensor(f"in_{name}", a.shape, mybir.dt.from_np(a.dtype), kind="ExternalInput").ap())
    out = nc.dram_tensor("out", arrays["in_x"].shape, F32, kind="ExternalOutput").ap()
    gnn_program(nc, *args, out)
    r = run_bass_kernel_spmd(nc, [arrays], core_ids=[0])
    return r.results[0]["out"]
```
